# Optimizing a Trainium2 kernel written in Bass

```python
import numpy as np
import jax
import jax.numpy as jnp

def _softmax(x, axis=-1):
    return jax.nn.softmax(x, axis=axis)

def _gelu(x):
    return jax.nn.gelu(x, approximate=True)

def _silu(x):
    return jax.nn.silu(x)

def _sigmoid(x):
    return jax.nn.sigmoid(x)

def _layernorm(x, axis=-1, eps=1e-05):
    m = jnp.mean(x, axis=axis, keepdims=True)
    v = jnp.var(x, axis=axis, keepdims=True)
    return (x - m) / jnp.sqrt(v + eps)

def _scatter_add(tgt, idx, src, axis=0):
    return tgt.at[idx].add(src)

def _segment_sum(src, seg, n):
    return jax.ops.segment_sum(src, seg, n)
kernel_name = 'mk_pixart_resid_d1_seqx_r8_b65e8d'

def setup_inputs(seed: int=0):
    np.random.seed(seed)
    _w = jnp.asarray

    def _rec_inputs():
        import jax
        import jax.numpy as jnp
        _rk = jax.random.key(seed)
        x = 7.22e-05 + 1 * jax.random.normal(jax.random.fold_in(_rk, 1), (4, 512, 128), jnp.float32)
        _lenS = 512 - jax.random.randint(jax.random.fold_in(_rk, 7), (4,), 0, max(1, 512 // 4) + 1, jnp.int32)
        _lenS2 = 77 - jax.random.randint(jax.random.fold_in(_rk, 8), (4,), 0, max(1, 77 // 4) + 1, jnp.int32)
        _ctx_1024P = jax.random.normal(jax.random.fold_in(_rk, 11), (4, 16, 128), jnp.float32)
        _ctx_1024c = jax.random.dirichlet(jax.random.fold_in(_rk, 511), 0.3 * jnp.ones((16,), jnp.float32), (4, 77))
        _ctx_1024t = jnp.einsum('bsk,bkd->bsd', _ctx_1024c, _ctx_1024P)
        _ctx_1024t = _ctx_1024t * jax.lax.rsqrt(jnp.mean(jnp.square(_ctx_1024t)) + 1e-12) * 0.953939
        ctx_1024 = 4.13588e-05 + 0.999923 * (_ctx_1024t + 0.3 * jax.random.normal(jax.random.fold_in(_rk, 611), (4, 77, 128), jnp.float32))
        condB_tau = jax.random.uniform(jax.random.fold_in(_rk, 12), (4,), jnp.float32, 0.0, 1.45372)
        fside_BxS2_0 = 0.0088954 + 1.00633 * jax.random.normal(jax.random.fold_in(_rk, 13), (4, 77), jnp.float32)
        return (x, ctx_1024, condB_tau, fside_BxS2_0)
    x, ctx_1024, condB_tau, fside_BxS2_0 = _rec_inputs()

    def _L0_xcond_setup():
        import jax, jax.numpy as jnp
        import numpy as np
        D_MODEL = 128
        N_HEADS = 16
        key = jax.random.key(seed)
        ks = jax.random.split(key, 16)
        B, L, S, D = (4, 256, 256, D_MODEL)
        inp = {'q': jax.random.normal(ks[0], (B, L, D), jnp.float32), 'k': jax.random.normal(ks[1], (B, S, D), jnp.float32), 'v': jax.random.normal(ks[2], (B, S, D), jnp.float32), 'tau': jax.random.uniform(ks[3], (B, 1), jnp.float32, 0.5, 1.5), 'delta': jax.random.normal(ks[4], (B, S), jnp.float32)}
        s = 1.0 / np.sqrt(D)
        inp['Wq'] = jax.random.normal(ks[5], (D, D), jnp.float32) * s
        inp['bq'] = jnp.zeros((D,), jnp.float32)
        inp['Wk'] = jax.random.normal(ks[6], (D, D), jnp.float32) * s
        inp['bk'] = jnp.zeros((D,), jnp.float32)
        inp['Wv'] = jax.random.normal(ks[7], (D, D), jnp.float32) * s
        inp['bv'] = jnp.zeros((D,), jnp.float32)
        inp['Wo'] = jax.random.normal(ks[8], (D, D), jnp.float32) * s
        inp['bo'] = jnp.zeros((D,), jnp.float32)
        return inp
    _L0_xcond_all = _L0_xcond_setup()
    _L0_xcond_in = {k: v for k, v in _L0_xcond_all.items() if k in ('Wq', 'bq', 'Wk', 'bk', 'Wv', 'bv', 'Wo', 'bo')}
    del _L0_xcond_all

    def _L0_ffn_setup():
        import jax, jax.numpy as jnp
        import numpy as np
        N_HEADS = 4
        key = jax.random.key(seed)
        k1, k2, k3, k4 = jax.random.split(key, 4)
        dmodel, n_experts, expert_size = (128, 64, 128)
        B, S = (4, 256)
        x = jax.random.normal(k1, (B, S, dmodel), dtype=jnp.float32)
        expert_sel = jax.random.normal(k2, (n_experts, dmodel), dtype=jnp.float32) * dmodel ** (-0.5)
        keys = jax.random.normal(k3, (n_experts, dmodel, expert_size), dtype=jnp.float32) * dmodel ** (-0.5)
        values = jax.random.normal(k4, (n_experts, expert_size, dmodel), dtype=jnp.float32) * (n_experts * expert_size) ** (-0.5)
        return {'x': x, 'expert_sel': expert_sel, 'keys': keys, 'values': values}
    _L0_ffn_all = _L0_ffn_setup()
    _L0_ffn_in = {k: v for k, v in _L0_ffn_all.items() if k in ('expert_sel', 'keys', 'values')}
    del _L0_ffn_all
    return {'x': x, 'ctx_1024': ctx_1024, 'condB_tau': condB_tau, 'fside_BxS2_0': fside_BxS2_0, 'L0_xcond_Wq': _L0_xcond_in['Wq'], 'L0_xcond_bq': _L0_xcond_in['bq'], 'L0_xcond_Wk': _L0_xcond_in['Wk'], 'L0_xcond_bk': _L0_xcond_in['bk'], 'L0_xcond_Wv': _L0_xcond_in['Wv'], 'L0_xcond_bv': _L0_xcond_in['bv'], 'L0_xcond_Wo': _L0_xcond_in['Wo'], 'L0_xcond_bo': _L0_xcond_in['bo'], 'L0_ffn_expert_sel': _L0_ffn_in['expert_sel'], 'L0_ffn_keys': _L0_ffn_in['keys'], 'L0_ffn_values': _L0_ffn_in['values']}

def reference(x, ctx_1024, condB_tau, fside_BxS2_0, L0_xcond_Wq, L0_xcond_bq, L0_xcond_Wk, L0_xcond_bk, L0_xcond_Wv, L0_xcond_bv, L0_xcond_Wo, L0_xcond_bo, L0_ffn_expert_sel, L0_ffn_keys, L0_ffn_values):
    import jax
    import jax.numpy as jnp

    def _L0_xcond_ref(q, k, v, tau, delta, Wq, bq, Wk, bk, Wv, bv, Wo, bo):
        import jax, jax.numpy as jnp
        import numpy as np
        D_MODEL = 128
        N_HEADS = 16
        B, L, D = q.shape
        S = k.shape[1]
        H = N_HEADS
        E = D // H
        qh = (q @ Wq.T + bq).reshape(B, L, H, E)
        kh = (k @ Wk.T + bk).reshape(B, S, H, E)
        vh = (v @ Wv.T + bv).reshape(B, S, H, E)
        scale = 1.0 / np.sqrt(E).astype(np.float32)
        scores = jnp.einsum('blhe,bshe->bhls', qh, kh)
        scores = scores * tau[:, None, None, :] + delta[:, None, None, :]
        a = jax.nn.softmax(scale * scores, axis=-1)
        out = jnp.einsum('bhls,bshd->blhd', a, vh).reshape(B, L, D)
        return out @ Wo.T + bo

    def _L0_ffn_ref(x, expert_sel, keys, values):
        import jax, jax.numpy as jnp
        import numpy as np
        N_HEADS = 4
        B, S, d = x.shape
        n_experts = keys.shape[0]
        xf = x.reshape(-1, d)
        N = xf.shape[0]
        logits = xf @ expert_sel.T
        sel = jax.nn.sigmoid(logits)
        sel_val, sel_idx = jax.lax.top_k(sel, N_HEADS)
        gates = jnp.zeros((N, n_experts), dtype=x.dtype)
        gates = gates.at[jnp.arange(N)[:, None], sel_idx].set(sel_val)
        h = jnp.einsum('nd,kde->nke', xf, keys)
        scores = jax.nn.relu(h) * gates[:, :, None]
        out = jnp.einsum('nke,kev->nv', scores, values)
        return out.reshape(B, S, -1)
    x = x + _L0_xcond_ref(_layernorm(x, axis=-1), ctx_1024, ctx_1024, condB_tau[:, None], fside_BxS2_0, L0_xcond_Wq, L0_xcond_bq, L0_xcond_Wk, L0_xcond_bk, L0_xcond_Wv, L0_xcond_bv, L0_xcond_Wo, L0_xcond_bo)
    x = x + _L0_ffn_ref(_layernorm(x, axis=-1), L0_ffn_expert_sel, L0_ffn_keys, L0_ffn_values)
    return x

_drawn_inputs = setup_inputs


def setup_inputs(seed=0):
    import zlib

    import numpy as np

    out = dict(_drawn_inputs(seed))
    spreads = {'L0_xcond_bq': (0.0, 0.283),
     'L0_xcond_bk': (0.0, 0.8),
     'L0_xcond_bv': (0.0, 0.1),
     'L0_xcond_bo': (0.0, 0.1)}
    factors = {}
    for name, (base, spread) in spreads.items():
        noise = np.random.default_rng([zlib.crc32(name.encode()), seed]).standard_normal(out[name].shape)
        drawn = base * np.exp(spread * noise) if base else spread * noise
        out[name] = jnp.asarray(drawn.astype(out[name].dtype))
    for name, factor in factors.items():
        out[name] = (out[name] * factor).astype(out[name].dtype)
    return out
```

```python
from contextlib import ExitStack

import concourse.bass as bass
from concourse import mybir

F32 = mybir.dt.float32
BF16 = mybir.dt.bfloat16
I32 = mybir.dt.int32
U32 = mybir.dt.uint32
ALU = mybir.AluOpType
ACT = mybir.ActivationFunctionType
AX = mybir.AxisListType

P = 128
B, L, D = 4, 512, 128
S = 77
H, E = 16, 8
HG = 4
NG = H // HG
R = HG * S
NC = (R + P - 1) // P
RP = NC * P
VW = HG * E + HG
T = L // P
NT = B * T
NE, TOPK = 64, 4
GROUPS = 2
BG = B // GROUPS
TG = T * BG
CAP = TG * TOPK + NE
CH = 4
NCH = GROUPS * CAP // CH
UN = 4
SCALE = 1.0 / float(E) ** 0.5
EPS = 1e-5
ZW = 8


def block_kernel(nc, x, ctx_in, tau, fside, Wq, bq, Wk, bk, Wv, bv, Wo, bo, esel, keys, values, out, xs, ys):
    xf = x.rearrange("b l d -> (b l) d")
    of = out.rearrange("b l d -> (b l) d")

    with ExitStack() as stack:
        def sb(name, shape, dt=F32):
            return stack.enter_context(nc.sbuf_tensor(name, shape, dt))

        def sem(name):
            return stack.enter_context(nc.semaphore(name))

        x_sb = sb("x_sb", [P, NT, D])
        x1_sb = x_sb
        xn2_sb = sb("xn2_sb", [P, NT, D])
        keys_sb = sb("keys_sb", [P, NE, P])
        vals_sb = sb("vals_sb", [P, NE, D])
        w_nat = sb("w_nat", [P, 4, D])
        wT = sb("wT", [P, 4, D])
        ctx_nat = sb("ctx_nat", [S, B, D])
        sel_nat = sb("sel_nat", [NE, D])
        selT = sb("selT", [P, NE])
        bq_col = sb("bq_col", [P, 1])
        bk_col = sb("bk_col", [P, 1])
        bv_bc = sb("bv_bc", [P, D])
        bo_bc = sb("bo_bc", [P, D])
        tau_bc = sb("tau_bc", [P, B])
        bqt = sb("bqt", [P, B])
        delta_bc = sb("delta_bc", [P, B, S])
        dcol = sb("dcol", [P, B, NC])
        dhi = sb("dhi", [P, B, S], BF16)
        dlo = sb("dlo", [P, B, S], BF16)
        dlm = sb("dlm", [P, B, S], BF16)
        dhl = sb("dhl", [P, B, S], BF16)
        KT = sb("KT", [P, B, S])
        Vb = sb("Vb", [P, B, NC, NG, VW])

        ident = sb("ident", [P, P])
        identb = sb("identb", [P, P], BF16)
        onesf = sb("onesf", [P, P])
        onesb = sb("onesb", [P, P], BF16)
        tri = sb("tri", [P, P], BF16)
        onev = sb("onev", [P, NC, HG])
        vm0 = sb("vm0", [P, NC, HG])
        vmask = sb("vmask", [P, NC, HG])
        pidx = sb("pidx", [P, 1], I32)
        pint = sb("pint", [P, 3], I32)
        pflt = sb("pflt", [P, 3])
        hrow = sb("hrow", [P, HG])
        hmask = sb("hmask", [P, HG])
        imask = sb("imask", [P, HG])
        ilt = sb("ilt", [P, 1])
        rm = sb("rm", [P, 2])
        ind = sb("ind", [P, RP], BF16)
        iota_e = sb("iota_e", [P, NE])
        jcol = sb("jcol", [P, 1])
        gbase = sb("gbase", [P, 1])
        zeros64 = sb("zeros64", [P, NE])
        mhalf = sb("mhalf", [P, T])
        zero = sb("zero", [P, ZW * D])

        st1 = sb("st1", [P, T, 6])
        mv1 = sb("mv1", [P, T, 2])
        ve1 = sb("ve1", [P, T])
        rs1 = sb("rs1", [P, T])
        xn1 = sb("xn1", [P, T, D])
        xnT = sb("xnT", [P, L])
        qT = [sb(f"qT{k}", [P, L]) for k in range(BG)]
        Kb = [sb(f"Kb{k}", [P, RP]) for k in range(BG)]
        dh4 = [sb(f"dh4{k}", [P, R], BF16) for k in range(BG)]
        mx = [sb(f"mx{k}", [P, T, H]) for k in range(BG)]
        negm = [sb(f"negm{k}", [P, T * NG, 32], BF16) for k in range(BG)]
        mT = [sb(f"mT{k}", [P, L], BF16) for k in range(BG)]
        PT = [sb(f"PT{k}", [P, NG * NC, L]) for k in range(BG)]
        rden = sb("rden", [P, 2 * NG, HG])
        att = sb("att", [P, T, D])
        aT = sb("aT", [P, L])
        xb = sb("xb", [P, T, D])
        st2 = sb("st2", [P, T, 6])
        mv2 = sb("mv2", [P, T, 2])
        ve2 = sb("ve2", [P, T])
        rs2 = sb("rs2", [P, T])
        xn2 = sb("xn2", [P, T, D])
        xn2T = sb("xn2T", [P, L])

        ex = sb("ex", [P, T, NE])
        wv = sb("wv", [P, T, NE])
        top = sb("top", [P, T, 8])
        tidx = sb("tidx", [P, T, 8], U32)
        tidf = sb("tidf", [P, T, 8])
        rgate = sb("rgate", [P, T, TOPK])
        gates = sb("gates", [P, NT * TOPK])
        OH = sb("OH", [P, TG, TOPK, NE])
        ctxT = OH[:].rearrange("p t k e -> p (t k e)")[:, 0:B * RP].rearrange("p (b r) -> p b r", b=B)
        oha = sb("oha", [P, T, 2, NE])
        mask = sb("mask", [P, TG, NE], BF16)
        cnt_i = sb("cnt_i", [P, NE], I32)
        cnt_t = sb("cnt_t", [P, NE], I32)
        ntile = sb("ntile", [P, NE])
        incl = sb("incl", [P, NE])
        excl = sb("excl", [P, NE])
        sbase = sb("sbase", [P, NE])
        pos = sb("pos", [P, TG, NE])
        slotf = sb("slotf", [P, TG * TOPK])
        slots = sb("slots", [P, NT * TOPK], I32)
        lecmp = sb("lecmp", [P, NE])
        ej = sb("ej", [P, 1])
        etab = sb("etab", [1, GROUPS * CAP], I32)

        pt0 = PT[0][:].rearrange("p v l -> p (v l)")
        pt1 = PT[1][:].rearrange("p v l -> p (v l)")
        vt = pt1[:, 0:B * NC * D].rearrange("p (b c d) -> p b c d", b=B, c=NC)
        drow = pt1[0:1, B * NC * D:B * NC * D + B * RP].rearrange("p (b r) -> p b r", b=B)
        gb = pt0[:, 0:TG * TOPK * D].rearrange("p (j d) -> p j d", d=D)
        room = [pt1[:, j * CH * P:(j + 1) * CH * P] for j in range(NG * NC)]
        xg = [room[k].rearrange("p (a d) -> p a d", a=CH) for k in range(UN)]
        xT, hr, hT, yb = room[4:6], room[6:8], room[8:10], room[10:12]
        ot = [sb(f"ot{k}", [P, D]) for k in range(2)]

        psA = [stack.enter_context(nc.psum_tensor(f"psA{k}", [P, 2, 512], F32)) for k in range(2)]
        psB = [stack.enter_context(nc.psum_tensor(f"psB{k}", [P, 512], F32)) for k in range(2)]
        psO = stack.enter_context(nc.psum_tensor("psO", [P, 512], F32))
        psM = stack.enter_context(nc.psum_tensor("psM", [P, 512], F32))
        mTp = psM[:, 0:256].bitcast(BF16)

        x_in, w_in, k_in, v_in = sem("x_in"), sem("w_in"), sem("k_in"), sem("v_in")
        zeroed = [sem(f"zeroed{g}") for g in range(GROUPS)]
        scattered = [sem(f"scattered{g}") for g in range(GROUPS)]
        names = """ones_set zero_set drow_zeroed ctxT_zeroed kb_zeroed negm_zeroed ident_set identb_set tri_set small_set
        vm0_set vmask_set pint_set pflt_set hrow_set hmask_set ilt_set imask_set ind_set rm_set iota_set
        wT_ps wT_sb ctxT_ps ctxT_sb selT_ps selT_sb kT_ps kT_sb v_ps vt_sb vb_set den_set drow_set dcol_ps dcol_sb bqt_set
        dhi_set dlo_set dlm_set dhl_set
        kb_ready dh4_ready xb_ready ln1_stats ln1_aggr ln1_eps ln1_rstd xn1_ready xnT_ps xnT_sb q_ps qT_sb
        a_ps max_done split_hi split_lo mT_ps mT_sb b_ps exp_done o_ps rden_done att_done aT_ps aT_sb y_ps x1_done
        ln2_stats ln2_aggr ln2_eps ln2_rstd xn2_done xn2_kept xn2T_ps xn2T_sb lg_ps ex_done w_done top_done idx_done
        tidf_done rgate_done gates_done oh_done oha_done mask_done route_ps cnt_done shift_done ntile_done incl_done
        excl_done base_done pos_done prod_done slotf_done slots_done ej_done ejT_ps etab_done step_done
        g_xT_ps g_xT_sb g_h_ps g_h_sb g_hT_ps g_hT_sb g_y_ps g_y_sb acc_done""".split()
        s = {n: sem(n) for n in names}
        xg_in = [sem(f"xg_in{k}") for k in range(UN)]
        y_out = [sem(f"y_out{k}") for k in range(2)]
        gb_in = [sem(f"gb_in{k}") for k in range(TG)]
        o_out = [sem(f"o_out{k}") for k in range(2)]
        NSMALL = 12

        def at(m, d=0):
            return m[0] + (m[1] + d)

        block = stack.enter_context(nc.Block())

        def load_rows(sp, m, k):
            sp.dma_start(xg[k], xs[bass.ds(at(m) * (CH * P), CH * P), :].rearrange("(a p) d -> p a d", p=P)
                         ).then_inc(xg_in[k], 16)

        def store_rows(sp, m, k):
            sp.wait_ge(s["g_y_sb"], at(m, 1))
            sp.dma_start(ys[bass.ds(at(m) * (CH * P), CH * P), :].rearrange("(a p) d -> p a d", p=P),
                         yb[k].rearrange("p (a d) -> p a d", a=CH)).then_inc(y_out[k], 16)

        @block.sync
        def _(sp):
            for j, w in enumerate((Wq, Wk, Wv, Wo)):
                sp.dma_start(w_nat[:, j], w).then_inc(w_in, 16)
            sp.dma_start(ctx_nat[:], ctx_in.rearrange("b s d -> s b d")).then_inc(w_in, 16)
            sp.dma_start(x_sb[:], xf.rearrange("(t p) d -> p t d", p=P)).then_inc(x_in, 16)
            sp.wait_ge(s["zero_set"], 1)
            zr = P * ZW
            half = GROUPS * CAP * P // GROUPS // zr
            for j in range(half):
                sp.dma_start(xs[j * zr:(j + 1) * zr, :].rearrange("(p r) d -> p (r d)", p=P), zero[:]).then_inc(zeroed[0], 16)
            sp.dma_start(keys_sb[:], keys.rearrange("e d k -> d e k")).then_inc(k_in, 16)
            sp.dma_start(vals_sb[:], values.rearrange("e k v -> k e v")).then_inc(v_in, 16)
            for j in range(half, GROUPS * half):
                sp.dma_start(xs[j * zr:(j + 1) * zr, :].rearrange("(p r) d -> p (r d)", p=P), zero[:]).then_inc(zeroed[1], 16)
            per = NCH // GROUPS
            sp.wait_ge(s["o_ps"], 2 * B)
            for g in range(GROUPS):
                sp.wait_ge(scattered[g], 16 * TG * TOPK)
                if g == 0:
                    for k in range(UN):
                        load_rows(sp, (0, k), k)
                    lo = 0
                else:
                    for k in range(UN):
                        m = g * per - UN + k
                        sp.wait_ge(s["g_xT_ps"], m + 1)
                        load_rows(sp, (0, m + UN), k)
                        store_rows(sp, (0, m), k % 2)
                    lo = g * per
                hi = (g + 1) * per - UN
                with sp.Fori(lo // UN, hi // UN) as r:
                    for k in range(UN):
                        sp.wait_ge(s["g_xT_ps"], r * UN + (k + 1))
                        load_rows(sp, (r * UN, k + UN), k)
                        store_rows(sp, (r * UN, k), k % 2)
            for k in range(UN):
                store_rows(sp, (0, NCH - UN + k), k % 2)
            with sp.Fori(0, NT // 2) as r:
                t0 = r * 2
                for k in range(2):
                    sp.wait_ge(s["acc_done"], t0 * TOPK + (k + 1) * TOPK)
                    sp.dma_start(of[bass.ds((t0 + k) * P, P), :], ot[k][:]).then_inc(o_out[k], 16)
            for k in range(2):
                sp.wait_ge(o_out[k], 16 * NT // 2)

        @block.gpsimd
        def _(pool):
            g = nc.gpsimd
            g.memset(onesf[:], 1.0).then_inc(s["ones_set"], 1)
            g.memset(onev[:], 1.0).then_inc(s["ones_set"], 1)
            g.memset(onesb[:], 1.0).then_inc(s["ones_set"], 1)
            g.iota(pidx[:], pattern=[[0, 1]], base=0, channel_multiplier=1).then_inc(s["iota_set"], 1)
            g.iota(iota_e[:], pattern=[[1, NE]], base=0, channel_multiplier=0,
                   allow_small_or_imprecise_dtypes=True).then_inc(s["iota_set"], 1)
            g.iota(jcol[:], pattern=[[0, 1]], base=0, channel_multiplier=1,
                   allow_small_or_imprecise_dtypes=True).then_inc(s["iota_set"], 1)
            g.iota(hrow[:], pattern=[[1, HG]], base=0, channel_multiplier=0,
                   allow_small_or_imprecise_dtypes=True).then_inc(s["iota_set"], 1)
            g.memset(mhalf[:], -0.5).then_inc(s["small_set"], 1)
            pool.wait_ge(s["ones_set"], 3)
            g.affine_select(out=ident[:], in_=onesf[:], pattern=[[-1, P]], compare_op=ALU.is_equal, fill=0.0,
                            base=0, channel_multiplier=1).then_inc(s["ident_set"], 1)
            g.memset(drow, 0.0).then_inc(s["drow_zeroed"], 1)
            g.memset(ctxT[:, :, R:RP], 0.0).then_inc(s["ctxT_zeroed"], 1)
            g.affine_select(out=identb[:], in_=onesb[:], pattern=[[-1, P]], compare_op=ALU.is_equal, fill=0.0,
                            base=0, channel_multiplier=1).then_inc(s["identb_set"], 1)
            g.affine_select(out=vm0[:], in_=onev[:], pattern=[[P, NC], [-S, HG]], compare_op=ALU.is_ge, fill=0.0,
                            base=0, channel_multiplier=1).then_inc(s["vm0_set"], 1)
            pool.wait_ge(s["vm0_set"], 1)
            g.affine_select(out=vmask[:], in_=vm0[:], pattern=[[-P, NC], [S, HG]], compare_op=ALU.is_ge, fill=0.0,
                            base=S - 1, channel_multiplier=-1).then_inc(s["vmask_set"], 1)
            for k in range(BG):
                g.memset(Kb[k][:, R:RP], 0.0).then_inc(s["kb_zeroed"], 1)
                g.memset(negm[k][:], 0.0).then_inc(s["negm_zeroed"], 1)
            g.affine_select(out=tri[:], in_=onesb[:], pattern=[[1, P]], compare_op=ALU.is_gt, fill=0.0,
                            base=0, channel_multiplier=-1).then_inc(s["tri_set"], 1)
            g.memset(zeros64[:], 0.0).then_inc(s["small_set"], 1)
            g.memset(gbase[:], 0.0).then_inc(s["small_set"], 1)
            pool.wait_ge(s["vmask_set"], 1)
            for c in range(NC):
                g.tensor_copy(Vb[:, :, c, :, HG * E:VW],
                              vmask[:, c:c + 1, :].rearrange("p a h -> p a () h").broadcast_to([P, B, NG, HG])
                              ).then_inc(s["den_set"], 1)

            def stage_kv(n, k):
                pool.wait_ge(s["kT_sb"], 1)
                pool.wait_ge(s["hmask_set"], 1)
                pool.wait_ge(s["dhl_set"], 1)
                if n >= BG:
                    pool.wait_ge(s["b_ps"], NG * NC * (n - BG + 1))
                g.tensor_tensor(Kb[k][:, 0:R].rearrange("p (h s) -> p h s", h=HG),
                                KT[:, n:n + 1, :].broadcast_to([P, HG, S]),
                                hmask[:].rearrange("p h -> p h ()").broadcast_to([P, HG, S]),
                                ALU.mult).then_inc(s["kb_ready"], 1)
                g.tensor_copy(dh4[k][:].rearrange("p (h s) -> p h s", h=HG),
                              dhl[:, n:n + 1, :].broadcast_to([P, HG, S])).then_inc(s["dh4_ready"], 1)

            def rstd(n, mv, ve, rs, aggr, eps, done):
                pool.wait_ge(s[aggr], n + 1)
                g.tensor_scalar(ve[:], mv[:, :, 1:2].rearrange("p t a -> p (t a)"), EPS, None, ALU.add).then_inc(s[eps], 1)
                pool.wait_ge(s[eps], n + 1)
                g.tensor_tensor(rs[:], ve[:], mhalf[:], ALU.pow).then_inc(s[done], 1)

            def add_bo(n):
                if n >= 1:
                    pool.wait_ge(s["x1_done"], n)
                g.tensor_tensor(xb[:], x_sb[:, n * T:(n + 1) * T, :],
                                bo_bc[:].rearrange("p d -> p () d").broadcast_to([P, T, D]), ALU.add
                                ).then_inc(s["xb_ready"], 1)

            def choice_masks(n, k):
                pool.wait_ge(s["xn2_done"], n + 1)
                g.tensor_copy(xn2_sb[:, n * T:(n + 1) * T, :], xn2[:]).then_inc(s["xn2_kept"], 1)
                pool.wait_ge(s["tidf_done"], n + 1)
                if n >= BG:
                    pool.wait_ge(s["slotf_done"], n // BG)
                for t in range(T):
                    for c in range(TOPK):
                        ins = g.tensor_scalar(OH[:, k * T + t, c, :], iota_e[:], tidf[:, t, c:c + 1], None, ALU.is_equal)
                ins.then_inc(s["oh_done"], 1)
                pool.wait_ge(s["oh_done"], n + 1)
                oh = OH[:, k * T:(k + 1) * T]
                g.tensor_tensor(oha[:], oh[:, :, 0:2, :], oh[:, :, 2:4, :], ALU.add).then_inc(s["oha_done"], 1)
                pool.wait_ge(s["oha_done"], n + 1)
                if n >= BG:
                    pool.wait_ge(s["route_ps"], n // BG)
                g.tensor_tensor(mask[:, k * T:(k + 1) * T, :], oha[:, :, 0, :], oha[:, :, 1, :], ALU.add
                                ).then_inc(s["mask_done"], 1)

            scatters = []

            def scatter(count):
                for _ in range(min(count, len(scatters))):
                    j = scatters.pop(0)
                    g.indirect_dma_start(out=xs[:, :], out_offset=bass.IndirectOffsetOnAxis(ap=slots[:, j:j + 1], axis=0),
                                         in_=xn2_sb[:, j // TOPK, :], in_offset=None).then_inc(scattered[j // (TG * TOPK)], 16)

            pool.wait_ge(x_in, 16)
            pool.wait_ge(w_in, 16 * NSMALL)
            for b in range(B):
                pool.wait_ge(s["vt_sb"], b + 1)
                for c in range(NC):
                    ins = g.tensor_tensor(Vb[:, b, c, :, 0:HG * E].rearrange("p g (h e) -> p g h e", h=HG),
                                          vt[:, b, c, :].rearrange("p (g h e) -> p g h e", g=NG, h=HG),
                                          vmask[:, c:c + 1, :].rearrange("p a h -> p a h ()").broadcast_to([P, NG, HG, E]),
                                          ALU.mult)
                ins.then_inc(s["vb_set"], 1)
            for i in range(GROUPS):
                b0, b1 = BG * i, BG * i + 1
                stage_kv(b0, 0)
                scatter(4)
                rstd(b0, mv1, ve1, rs1, "ln1_aggr", "ln1_eps", "ln1_rstd")
                stage_kv(b1, 1)
                scatter(4)
                rstd(b1, mv1, ve1, rs1, "ln1_aggr", "ln1_eps", "ln1_rstd")
                add_bo(b0)
                scatter(12)
                rstd(b0, mv2, ve2, rs2, "ln2_aggr", "ln2_eps", "ln2_rstd")
                choice_masks(b0, 0)
                add_bo(b1)
                scatter(12)
                rstd(b1, mv2, ve2, rs2, "ln2_aggr", "ln2_eps", "ln2_rstd")
                choice_masks(b1, 1)
                scatter(len(scatters))
                pool.wait_ge(s["slots_done"], i + 1)
                pool.wait_ge(s["xn2_kept"], BG * (i + 1))
                pool.wait_ge(zeroed[i], 16 * CAP // ZW)
                scatters += [i * TG * TOPK + j for j in range(TG * TOPK)]
            scatter(len(scatters))

            for j in range(NT * TOPK):
                if j % (TG * TOPK) == 0:
                    grp = j // (TG * TOPK)
                    for k in range(2):
                        pool.wait_ge(y_out[k], 16 * NCH // 2 // GROUPS * (grp + 1))
                if j >= TG * TOPK:
                    pool.wait_ge(s["acc_done"], j - TG * TOPK + 1)
                g.indirect_dma_start(out=gb[:, j % (TG * TOPK), :], out_offset=None, in_=ys[0:(grp + 1) * CAP * P, :],
                                     in_offset=bass.IndirectOffsetOnAxis(ap=slots[:, j:j + 1], axis=0)
                                     ).then_inc(gb_in[j // TOPK % TG], 16)

        @block.scalar
        def _(act):
            a = nc.scalar
            with nc.allow_non_contiguous_dma(reason="bias columns and broadcast rows, small"):
                act.dma_start(sel_nat[:], esel).then_inc(w_in, 16)
                act.dma_start(bq_col[:], bq.rearrange("(p a) -> p a", a=1)).then_inc(w_in, 16)
                act.dma_start(bk_col[:], bk.rearrange("(p a) -> p a", a=1)).then_inc(w_in, 16)
                act.dma_start(bv_bc[:], bv.rearrange("(a d) -> a d", a=1).broadcast_to([P, D])).then_inc(w_in, 16)
                act.dma_start(bo_bc[:], bo.rearrange("(a d) -> a d", a=1).broadcast_to([P, D])).then_inc(w_in, 16)
                act.dma_start(tau_bc[:], tau.rearrange("(a d) -> a d", a=1).broadcast_to([P, B])).then_inc(w_in, 16)
                act.dma_start(delta_bc[:], fside.rearrange("(a b) s -> a b s", a=1).broadcast_to([P, B, S])).then_inc(w_in, 16)
            act.wait_ge(s["wT_ps"], 1)
            a.copy(wT[:].rearrange("p j d -> p (j d)"), psB[0][:]).then_inc(s["wT_sb"], 1)

            def copy_xnT(n, k):
                act.wait_ge(s["xnT_ps"], n + 1)
                a.copy(xnT[:], psM[:]).then_inc(s["xnT_sb"], 1)

            def scale_q(n, k):
                act.wait_ge(s["q_ps"], n + 1)
                a.activation(qT[k][:], psM[:], ACT.Identity, bias=bqt[:, bass.ds(n, 1)],
                             scale=tau_bc[:, bass.ds(n, 1)]).then_inc(s["qT_sb"], 1)

            def copy_mT(n, k):
                act.wait_ge(s["mT_ps"], n + 1)
                a.copy(mT[k][:], mTp).then_inc(s["mT_sb"], 1)

            def exps(n, k, v0, v1):
                for v in range(v0, v1):
                    c = v % NC
                    act.wait_ge(s["b_ps"], NG * NC * n + v + 1)
                    a.activation(PT[k][:, v, :], psB[v % 2][:], ACT.Exp,
                                 bias=dcol[:, bass.ds(n, 1), c:c + 1].rearrange("p a b -> p (a b)"),
                                 scale=SCALE).then_inc(s["exp_done"], 1)

            def copy_aT(n, k):
                act.wait_ge(s["aT_ps"], n + 1)
                a.copy(aT[:], psM[:]).then_inc(s["aT_sb"], 1)

            def copy_xn2T(n, k):
                act.wait_ge(s["xn2T_ps"], n + 1)
                a.copy(xn2T[:], psM[:]).then_inc(s["xn2T_sb"], 1)

            def exp_logits(n, k):
                act.wait_ge(s["lg_ps"], n + 1)
                if n:
                    act.wait_ge(s["w_done"], n)
                a.activation(ex[:].rearrange("p t e -> p (t e)"), psM[:, 0:T * NE], ACT.Exp,
                             scale=-1.0).then_inc(s["ex_done"], 1)

            act.wait_ge(s["bqt_set"], 1)
            act.wait_ge(s["dcol_sb"], 1)
            for i in range(GROUPS):
                b0 = i * BG
                b1 = i * BG + 1
                copy_xnT(b0, 0)
                scale_q(b0, 0)
                copy_mT(b0, 0)
                exps(b0, 0, 0, 2)
                copy_xnT(b1, 1)
                scale_q(b1, 1)
                exps(b0, 0, 2, NG * NC)
                copy_mT(b1, 1)
                exps(b1, 1, 0, 4)
                copy_aT(b0, 0)
                exps(b1, 1, 4, 7)
                copy_xn2T(b0, 0)
                exps(b1, 1, 7, 10)
                exp_logits(b0, 0)
                exps(b1, 1, 10, NG * NC)
                copy_aT(b1, 1)
                copy_xn2T(b1, 1)
                exp_logits(b1, 1)

            def copy_gxT(m, k):
                act.wait_ge(s["g_xT_ps"], at(m, 1))
                a.copy(xT[k], psA[0][:, k, :]).then_inc(s["g_xT_sb"], 1)

            def copy_ghT(m, k):
                act.wait_ge(s["g_hT_ps"], at(m, 1))
                a.copy(hT[k], psB[k][:]).then_inc(s["g_hT_sb"], 1)

            copy_gxT((0, 0), 0)
            copy_gxT((0, 1), 1)
            copy_ghT((0, 0), 0)
            with act.Fori(0, (NCH - 2) // 2) as r:
                for k in range(2):
                    copy_gxT((r * 2, k + 2), k)
                    copy_ghT((r * 2, k + 1), (k + 1) % 2)
            copy_ghT((0, NCH - 1), (NCH - 1) % 2)

        @block.vector
        def _(dve):
            v = nc.vector
            v.memset(zero[:], 0.0).then_inc(s["zero_set"], 1)
            dve.wait_ge(s["iota_set"], 4)
            v.tensor_scalar(pint[:, 0:1], pidx[:], 3, 3, ALU.logical_shift_right, ALU.bitwise_and).then_inc(s["pint_set"], 1)
            v.tensor_scalar(pint[:, 1:2], pidx[:], 31, None, ALU.bitwise_and).then_inc(s["pint_set"], 1)
            v.tensor_scalar(pint[:, 2:3], pidx[:], 3, None, ALU.bitwise_and).then_inc(s["pint_set"], 1)
            dve.wait_ge(s["pint_set"], 3)
            v.tensor_copy(pflt[:], pint[:]).then_inc(s["pflt_set"], 1)
            dve.wait_ge(s["pflt_set"], 1)
            v.tensor_scalar(hmask[:], hrow[:], pflt[:, 0:1], None, ALU.is_equal).then_inc(s["hmask_set"], 1)
            v.tensor_scalar(ilt[:], pflt[:, 1:2], 8.0, None, ALU.is_lt).then_inc(s["ilt_set"], 1)
            v.tensor_scalar(rm[:, 0:1], pflt[:, 1:2], 0.0, None, ALU.is_equal).then_inc(s["rm_set"], 1)
            v.tensor_scalar(rm[:, 1:2], pflt[:, 1:2], 1.0, None, ALU.is_equal).then_inc(s["rm_set"], 1)
            dve.wait_ge(s["ilt_set"], 1)
            v.tensor_scalar(imask[:], hrow[:], pflt[:, 2:3], ilt[:, 0:1], ALU.is_equal, ALU.mult).then_inc(s["imask_set"], 1)
            v.memset(ind[:, R:RP], 0.0).then_inc(s["ind_set"], 1)
            dve.wait_ge(s["imask_set"], 1)
            v.tensor_copy(ind[:, 0:R].rearrange("p (h s) -> p h s", h=HG),
                          imask[:].rearrange("p h -> p h ()").broadcast_to([P, HG, S])).then_inc(s["ind_set"], 1)

            def ln_stats(n, src, st, stats):
                for t in range(T):
                    ins = v.bn_stats(st[:, t, :], src(n, t))
                ins.then_inc(s[stats], 1)

            def ln_aggr(n, st, mv, stats, aggr):
                dve.wait_ge(s[stats], n + 1)
                for t in range(T):
                    ins = v.bn_aggr(mv[:, t, :], st[:, t, :])
                ins.then_inc(s[aggr], 1)

            def ln_apply(n, src, dst, mv, rs, aggr, rstd_sem, done):
                dve.wait_ge(s[aggr], n + 1)
                dve.wait_ge(s[rstd_sem], n + 1)
                for t in range(T):
                    ins = v.tensor_scalar(dst[:, t, :], src(n, t), mv[:, t, 0:1], rs[:, t:t + 1], ALU.subtract, ALU.mult)
                ins.then_inc(s[done], 1)

            def x_tile(n, t):
                return x_sb[:, bass.ds(n * T + t, 1), :].rearrange("p a d -> p (a d)")

            def x1_tile(n, t):
                return x1_sb[:, bass.ds(n * T + t, 1), :].rearrange("p a d -> p (a d)")

            def norm1(n):
                ln_stats(n, x_tile, st1, "ln1_stats")
                ln_aggr(n, st1, mv1, "ln1_stats", "ln1_aggr")
                if n:
                    dve.wait_ge(s["xnT_ps"], n)
                ln_apply(n, x_tile, xn1, mv1, rs1, "ln1_aggr", "ln1_rstd", "xn1_ready")

            def maxima(n, k, u0, u1):
                for u in range(u0, u1):
                    t, p = u // 2, u % 2
                    dve.wait_ge(s["a_ps"], 2 * T * n + u + 1)
                    v.tensor_reduce(mx[k][:, t, 8 * p:8 * p + 8].rearrange("p (a h) -> p a h", a=2),
                                    psA[p][:, :, 0:R].rearrange("p a (h s) -> p a h s", h=HG),
                                    AX.X, ALU.max).then_inc(s["max_done"], 1)

            def split_max(n, k):
                dve.wait_ge(s["max_done"], 2 * T * (n + 1))
                m = mx[k][:].rearrange("p t (g h) -> p (t g) h", g=NG)
                v.tensor_scalar(negm[k][:, :, 0:HG], m, -1.0, None, ALU.mult).then_inc(s["split_hi"], 1)
                dve.wait_ge(s["split_hi"], n + 1)
                v.scalar_tensor_tensor(out=negm[k][:, :, HG:2 * HG], in0=m, scalar=-1.0, in1=negm[k][:, :, 0:HG],
                                       op0=ALU.mult, op1=ALU.subtract).then_inc(s["split_lo"], 1)

            def normalise(n, half):
                dve.wait_ge(s["o_ps"], 2 * n + half + 1)
                o = psO[:, 0:2 * NG * VW].rearrange("p (g w) -> p g w", w=VW)
                v.reciprocal(rden[:], o[:, :, HG * E:VW]).then_inc(s["rden_done"], 1)
                dve.wait_ge(s["rden_done"], 2 * n + half + 1)
                v.tensor_tensor(att[:, 2 * half:2 * half + 2, :].rearrange("p t (g h e) -> p (t g) h e", g=NG, h=HG),
                                o[:, :, 0:HG * E].rearrange("p g (h e) -> p g h e", h=HG),
                                rden[:].rearrange("p g h -> p g h ()").broadcast_to([P, 2 * NG, HG, E]),
                                ALU.mult).then_inc(s["att_done"], 1)

            def residual(n):
                dve.wait_ge(s["y_ps"], n + 1)
                dve.wait_ge(s["xb_ready"], n + 1)
                v.tensor_tensor(x1_sb[:, bass.ds(n * T, T), :], psM[:].rearrange("p (t d) -> p t d", t=T), xb[:],
                                ALU.add).then_inc(s["x1_done"], 1)

            def norm2(n):
                dve.wait_ge(s["x1_done"], n + 1)
                ln_stats(n, x1_tile, st2, "ln2_stats")
                ln_aggr(n, st2, mv2, "ln2_stats", "ln2_aggr")
                if n:
                    dve.wait_ge(s["xn2T_ps"], n)
                    dve.wait_ge(s["xn2_kept"], n)
                ln_apply(n, x1_tile, xn2, mv2, rs2, "ln2_aggr", "ln2_rstd", "xn2_done")

            def choose(n):
                dve.wait_ge(s["ex_done"], n + 1)
                v.tensor_scalar(wv[:], ex[:], -1.0, -1.0, ALU.mult, ALU.add).then_inc(s["w_done"], 1)
                dve.wait_ge(s["w_done"], n + 1)
                for t in range(T):
                    ins = v.max(top[:, t, :], wv[:, t, :])
                ins.then_inc(s["top_done"], 1)
                dve.wait_ge(s["top_done"], n + 1)
                for t in range(T):
                    ins = v.max_index(tidx[:, t, :], top[:, t, :], wv[:, t, :])
                ins.then_inc(s["idx_done"], 1)
                v.reciprocal(rgate[:], top[:, :, 0:TOPK]).then_inc(s["rgate_done"], 1)
                dve.wait_ge(s["idx_done"], n + 1)
                if n:
                    dve.wait_ge(s["mask_done"], n)
                v.tensor_copy(tidf[:], tidx[:]).then_inc(s["tidf_done"], 1)
                dve.wait_ge(s["rgate_done"], n + 1)
                v.tensor_scalar(gates[:, bass.ds(n * (T * TOPK), T * TOPK)], rgate[:].rearrange("p t k -> p (t k)"),
                                -1.0, None, ALU.mult).then_inc(s["gates_done"], 1)

            def route(i):
                dve.wait_ge(s["route_ps"], i + 1)
                v.tensor_scalar(cnt_i[:], psM[:, 0:NE], float(P - 1), None, ALU.add).then_inc(s["cnt_done"], 1)
                dve.wait_ge(s["cnt_done"], i + 1)
                v.tensor_scalar(cnt_t[:], cnt_i[:], 7, None, ALU.logical_shift_right).then_inc(s["shift_done"], 1)
                dve.wait_ge(s["shift_done"], i + 1)
                v.tensor_copy(ntile[:], cnt_t[:]).then_inc(s["ntile_done"], 1)
                dve.wait_ge(s["ntile_done"], i + 1)
                v.tensor_tensor_scan(incl[:], ntile[:], zeros64[:], gbase[:, 0:1], ALU.add, ALU.add).then_inc(s["incl_done"], 1)
                dve.wait_ge(s["incl_done"], i + 1)
                v.tensor_tensor(excl[:], incl[:], ntile[:], ALU.subtract).then_inc(s["excl_done"], 1)
                dve.wait_ge(s["excl_done"], i + 1)
                v.tensor_scalar(sbase[:], excl[:], float(P), None, ALU.mult).then_inc(s["base_done"], 1)
                dve.wait_ge(s["base_done"], i + 1)
                v.tensor_tensor(pos[:], psO[:].rearrange("p (t e) -> p t e", t=TG),
                                sbase[:].rearrange("p e -> p () e").broadcast_to([P, TG, NE]), ALU.add
                                ).then_inc(s["pos_done"], 1)
                dve.wait_ge(s["pos_done"], i + 1)
                v.tensor_tensor(OH[:], OH[:], pos[:].rearrange("p t e -> p t () e").broadcast_to([P, TG, TOPK, NE]),
                                ALU.mult).then_inc(s["prod_done"], 1)
                dve.wait_ge(s["prod_done"], i + 1)
                v.tensor_reduce(slotf[:], OH[:].rearrange("p t k e -> p (t k) e"), AX.X, ALU.add).then_inc(s["slotf_done"], 1)
                dve.wait_ge(s["slotf_done"], i + 1)
                v.tensor_copy(slots[:, bass.ds(i * (TG * TOPK), TG * TOPK)], slotf[:]).then_inc(s["slots_done"], 1)
                v.tensor_scalar(lecmp[0:CAP, :], incl[0:CAP, :], jcol[0:CAP, 0:1], 0.0, ALU.is_le, ALU.add,
                                accum_out=ej[0:CAP, :]).then_inc(s["ej_done"], 1)
                dve.wait_ge(s["ej_done"], i + 1)
                v.tensor_scalar(jcol[:], jcol[:], float(CAP), None, ALU.add).then_inc(s["step_done"], 1)
                v.tensor_scalar(gbase[:], gbase[:], float(CAP), None, ALU.add).then_inc(s["step_done"], 1)
                dve.wait_ge(s["ejT_ps"], i + 1)
                dve.wait_ge(s["step_done"], 2 * i + 2)
                v.tensor_scalar(etab[0:1, bass.ds(i * CAP, CAP)], psM[0:1, 128:128 + CAP], float(NE - 1), None,
                                ALU.min).then_inc(s["etab_done"], 1)

            dve.wait_ge(x_in, 16)
            dve.wait_ge(w_in, 16 * NSMALL)
            dve.wait_ge(s["ctxT_ps"], 1)
            v.tensor_copy(ctxT[:, :, 0:R].rearrange("p b (h s) -> p b h s", h=HG),
                          psA[0][:, 0, 0:B * S].rearrange("p (b s) -> p b () s", b=B).broadcast_to([P, B, HG, S])
                          ).then_inc(s["ctxT_sb"], 1)
            dve.wait_ge(s["drow_zeroed"], 1)
            v.tensor_copy(drow[:, :, 0:R].rearrange("p b (h s) -> p b h s", h=HG),
                          delta_bc[0:1].rearrange("p b s -> p b () s").broadcast_to([1, B, HG, S])).then_inc(s["drow_set"], 1)
            v.tensor_scalar(bqt[:], tau_bc[:], bq_col[:, 0:1], None, ALU.mult).then_inc(s["bqt_set"], 1)
            dve.wait_ge(s["kT_ps"], 1)
            v.tensor_scalar(KT[:].rearrange("p b s -> p (b s)"), psA[0][:, 1, 0:B * S], bk_col[:, 0:1], None,
                            ALU.add).then_inc(s["kT_sb"], 1)
            v.tensor_copy(dhi[:], delta_bc[:]).then_inc(s["dhi_set"], 1)
            dve.wait_ge(s["dhi_set"], 1)
            v.tensor_tensor(dlo[:], delta_bc[:], dhi[:], ALU.subtract).then_inc(s["dlo_set"], 1)
            dve.wait_ge(s["dlo_set"], 1)
            dve.wait_ge(s["rm_set"], 2)
            v.tensor_scalar(dlm[:], dlo[:], rm[:, 1:2], None, ALU.mult).then_inc(s["dlm_set"], 1)
            dve.wait_ge(s["dlm_set"], 1)
            v.scalar_tensor_tensor(out=dhl[:].rearrange("p b s -> p (b s)"), in0=dhi[:].rearrange("p b s -> p (b s)"),
                                   scalar=rm[:, 0:1], in1=dlm[:].rearrange("p b s -> p (b s)"),
                                   op0=ALU.mult, op1=ALU.add).then_inc(s["dhl_set"], 1)
            dve.wait_ge(s["selT_ps"], 1)
            v.tensor_copy(selT[:], psO[:, 0:NE]).then_inc(s["selT_sb"], 1)
            dve.wait_ge(s["dcol_ps"], 1)
            v.tensor_scalar(dcol[:].rearrange("p b c -> p (b c)"), psO[:, 128:128 + B * NC], SCALE, None,
                            ALU.mult).then_inc(s["dcol_sb"], 1)
            for b in range(B):
                dve.wait_ge(s["v_ps"], b + 1)
                src = (psA[1][:, 0], psA[1][:, 1], psB[0], psB[1])[b]
                v.tensor_tensor(vt[:, b], src[:, 0:NC * D].rearrange("p (c d) -> p c d", c=NC),
                                bv_bc[:].rearrange("p d -> p () d").broadcast_to([P, NC, D]), ALU.add
                                ).then_inc(s["vt_sb"], 1)

            dve.wait_ge(s["negm_zeroed"], BG)
            for i in range(GROUPS):
                b0 = i * BG
                b1 = i * BG + 1
                norm1(b0)
                maxima(b0, 0, 0, 2 * T)
                split_max(b0, 0)
                norm1(b1)
                maxima(b1, 1, 0, 2 * T)
                split_max(b1, 1)
                normalise(b0, 0)
                normalise(b0, 1)
                residual(b0)
                norm2(b0)
                choose(b0)
                normalise(b1, 0)
                normalise(b1, 1)
                residual(b1)
                norm2(b1)
                choose(b1)
                route(i)

            def relu_hidden(m, k):
                dve.wait_ge(s["g_h_ps"], at(m, 1))
                v.tensor_scalar(hr[k], psA[1][:, k, :], 0.0, None, ALU.max).then_inc(s["g_h_sb"], 1)

            def copy_out(m, k, stored):
                dve.wait_ge(s["g_y_ps"], at(m, 1))
                if stored is not None:
                    dve.wait_ge(y_out[k], stored)
                v.tensor_copy(yb[k], (psO, psM)[k][:]).then_inc(s["g_y_sb"], 1)

            relu_hidden((0, 0), 0)
            relu_hidden((0, 1), 1)
            copy_out((0, 0), 0, None)
            relu_hidden((0, 2), 0)
            copy_out((0, 1), 1, None)
            with dve.Fori(1, (NCH - 2) // 2) as r:
                for k in range(2):
                    relu_hidden((r * 2, k + 1), (1 + k) % 2)
                    copy_out((r * 2, k), k, r * 16)
            relu_hidden((0, NCH - 1), (NCH - 1) % 2)
            copy_out((0, NCH - 2), 0, (NCH - 2) * 8)
            copy_out((0, NCH - 1), 1, (NCH - 2) * 8)

            for i in range(GROUPS):
                for t in range(TG):
                    dve.wait_ge(gb_in[t], (i + 1) * (16 * TOPK))
                    if i or t >= 2:
                        dve.wait_ge(o_out[t % 2], i * (16 * TG // 2) + 16 * (t // 2))
                    for c in range(TOPK):
                        j = i * (TG * TOPK) + (t * TOPK + c)
                        if c:
                            dve.wait_ge(s["acc_done"], j)
                        prev = ot[t % 2][:] if c else x1_sb[:, bass.ds(i * TG + t, 1), :].rearrange("p a d -> p (a d)")
                        v.scalar_tensor_tensor(out=ot[t % 2][:], in0=gb[:, t * TOPK + c, :], scalar=gates[:, bass.ds(j, 1)],
                                               in1=prev, op0=ALU.mult, op1=ALU.add).then_inc(s["acc_done"], 1)

        @block.tensor
        def _(pe):
            t_ = nc.tensor

            pe.wait_ge(w_in, 16 * NSMALL)
            pe.wait_ge(s["ident_set"], 1)
            for b in range(B):
                ins = t_.transpose(psA[0][:, 0, b * S:(b + 1) * S], ctx_nat[:, b, :], ident[0:S, 0:S])
            ins.then_inc(s["ctxT_ps"], 1)
            for j in range(4):
                ins = t_.transpose(psB[0][:, j * D:(j + 1) * D], w_nat[:, j, :], ident[:])
            ins.then_inc(s["wT_ps"], 1)
            t_.transpose(psO[:, 0:NE], sel_nat[:], ident[0:NE, 0:NE]).then_inc(s["selT_ps"], 1)
            pe.wait_ge(s["wT_sb"], 1)
            pe.wait_ge(s["ctxT_sb"], 1)
            t_.matmul(psA[0][:, 1, 0:B * S].rearrange("p (b s) -> p b s", b=B), wT[:, 1, :], ctxT[:, :, 0:S],
                      start=True, stop=True).then_inc(s["kT_ps"], 1)
            pe.wait_ge(s["selT_sb"], 1)
            pe.wait_ge(s["drow_set"], 1)
            for b in range(B):
                for c in range(NC):
                    ins = t_.matmul(psO[:, 128 + b * NC + c:129 + b * NC + c], drow[0:1, b, c * P:(c + 1) * P],
                                    onesf[0:1, 0:1], start=True, stop=True)
            ins.then_inc(s["dcol_ps"], 1)
            pe.wait_ge(s["ctxT_zeroed"], 1)
            for b in range(B):
                dst = (psA[1][:, 0], psA[1][:, 1], psB[0], psB[1])[b]
                for c in range(NC):
                    ins = t_.matmul(dst[:, c * D:(c + 1) * D], ctxT[:, b, c * P:(c + 1) * P], wT[:, 2, :],
                                    start=True, stop=True)
                ins.then_inc(s["v_ps"], 1)

            def transposes(src, done):
                for t in range(T):
                    ins = t_.transpose(psM[:, t * P:(t + 1) * P], src[:, t, :], ident[:])
                ins.then_inc(s[done], 1)

            def project_q(n):
                pe.wait_ge(s["xn1_ready"], n + 1)
                transposes(xn1, "xnT_ps")
                pe.wait_ge(s["xnT_sb"], n + 1)
                t_.matmul(psM[:], wT[:, 0, :], xnT[:], start=True, stop=True).then_inc(s["q_ps"], 1)

            def scores_for_max(n, k, u):
                t, p = u // 2, u % 2
                if u == 0:
                    pe.wait_ge(s["qT_sb"], n + 1)
                    pe.wait_ge(s["kb_ready"], n + 1)
                    pe.wait_ge(s["dh4_ready"], n + 1)
                if u >= 2:
                    pe.wait_ge(s["max_done"], 2 * T * n + u - 1)
                elif n:
                    pe.wait_ge(s["max_done"], 2 * T * n)
                for a in range(2):
                    r = slice(32 * (2 * p + a), 32 * (2 * p + a) + 32)
                    t_.matmul(psA[p][:, a, 0:R], qT[k][r, t * P:(t + 1) * P], Kb[k][r, 0:R], start=True, stop=False)
                    ins = t_.matmul(psA[p][:, a, 0:R], onesb[r, :], dh4[k][r, :], start=False, stop=True)
                ins.then_inc(s["a_ps"], 1)

            def shift_rows(n, k):
                pe.wait_ge(s["split_lo"], n + 1)
                pe.wait_ge(s["qT_sb"], n + 1)
                for t in range(T):
                    ins = t_.transpose(mTp[:, t * P:(t + 1) * P],
                                       negm[k][:, t * NG:(t + 1) * NG, :].rearrange("p g j -> p (g j)"), identb[:])
                ins.then_inc(s["mT_ps"], 1)

            def scores(n, k, v0, v1):
                if v0 == 0:
                    pe.wait_ge(s["mT_sb"], n + 1)
                for v in range(v0, v1):
                    g, c = v // NC, v % NC
                    r = slice(32 * g, 32 * g + 32)
                    if n or v >= 2:
                        pe.wait_ge(s["exp_done"], NG * NC * n + max(v - 1, 0))
                    t_.matmul(psB[v % 2][:], Kb[k][r, c * P:(c + 1) * P], qT[k][r, :], start=True, stop=False)
                    t_.matmul(psB[v % 2][:], ind[r, c * P:(c + 1) * P], mT[k][r, :], start=False, stop=True
                              ).then_inc(s["b_ps"], 1)

            def attend(n, k, half):
                if half == 0:
                    pe.wait_ge(s["exp_done"], NG * NC * (n + 1))
                if n or half:
                    pe.wait_ge(s["att_done"], 2 * n + half)
                for a in range(2):
                    t = 2 * half + a
                    for g in range(NG):
                        o = (a * NG + g) * VW
                        for c in range(NC):
                            ins = t_.matmul(psO[:, o:o + VW], PT[k][:, g * NC + c, t * P:(t + 1) * P],
                                            Vb[:, bass.ds(n, 1), c, g, :].rearrange("p a w -> p (a w)"),
                                            start=(c == 0), stop=(c == NC - 1))
                ins.then_inc(s["o_ps"], 1)

            def turn_attention(n):
                pe.wait_ge(s["att_done"], 2 * n + 2)
                transposes(att, "aT_ps")

            def project_out(n):
                pe.wait_ge(s["aT_sb"], n + 1)
                for t in range(T):
                    ins = t_.matmul(psM[:, t * D:(t + 1) * D], aT[:, t * P:(t + 1) * P], wT[:, 3, :], start=True, stop=True)
                ins.then_inc(s["y_ps"], 1)

            def turn_xn2(n):
                pe.wait_ge(s["xn2_done"], n + 1)
                pe.wait_ge(s["x1_done"], n + 1)
                transposes(xn2, "xn2T_ps")

            def logits(n):
                pe.wait_ge(s["xn2T_sb"], n + 1)
                for t in range(T):
                    ins = t_.matmul(psM[:, t * NE:(t + 1) * NE], xn2T[:, t * P:(t + 1) * P], selT[:], start=True, stop=True)
                ins.then_inc(s["lg_ps"], 1)

            def count(i):
                pe.wait_ge(s["mask_done"], BG * (i + 1))
                po = psO[:].rearrange("p (t e) -> p t e", e=NE)
                t_.matmul(po, tri[:], mask[:], start=True, stop=False)
                for t in range(TG - 1):
                    t_.matmul(po[:, t + 1:TG, :], onesb[:], mask[:, t:t + 1, :].broadcast_to([P, TG - 1 - t, NE]),
                              start=False, stop=(t == TG - 2))
                pe.wait_ge(s["ex_done"], BG * (i + 1))
                for t in range(TG):
                    ins = t_.matmul(psM[:, 0:NE], onesb[:], mask[:, t, :], start=(t == 0), stop=(t == TG - 1))
                ins.then_inc(s["route_ps"], 1)

            pe.wait_ge(s["vt_sb"], B)
            pe.wait_ge(s["dcol_sb"], 1)
            pe.wait_ge(s["kb_zeroed"], BG)
            pe.wait_ge(s["ind_set"], 2)
            pe.wait_ge(s["identb_set"], 1)
            pe.wait_ge(s["vb_set"], B)
            pe.wait_ge(s["den_set"], NC)
            pe.wait_ge(s["tri_set"], 1)
            for i in range(GROUPS):
                b0 = i * BG
                b1 = i * BG + 1
                if i:
                    pe.wait_ge(s["etab_done"], i)
                project_q(b0)
                for u in range(2 * T):
                    scores_for_max(b0, 0, u)
                shift_rows(b0, 0)
                scores(b0, 0, 0, 2)
                pe.wait_ge(s["mT_sb"], b0 + 1)
                project_q(b1)
                for u in range(2 * T):
                    scores(b0, 0, 2 + u, 3 + u)
                    scores_for_max(b1, 1, u)
                scores(b0, 0, 2 + 2 * T, NG * NC)
                shift_rows(b1, 1)
                scores(b1, 1, 0, 2)
                if i:
                    pe.wait_ge(s["pos_done"], i)
                attend(b0, 0, 0)
                scores(b1, 1, 2, 4)
                attend(b0, 0, 1)
                pe.wait_ge(s["mT_sb"], b1 + 1)
                turn_attention(b0)
                scores(b1, 1, 4, 6)
                project_out(b0)
                scores(b1, 1, 6, 7)
                turn_xn2(b0)
                scores(b1, 1, 7, 9)
                logits(b0)
                scores(b1, 1, 9, NG * NC)
                attend(b1, 1, 0)
                attend(b1, 1, 1)
                pe.wait_ge(s["ex_done"], b0 + 1)
                turn_attention(b1)
                project_out(b1)
                turn_xn2(b1)
                logits(b1)
                count(i)
                pe.wait_ge(s["ej_done"], i + 1)
                t_.matmul(psM[0:1, P:P + CAP], ej[0:CAP, 0:1], ident[0:CAP, 0:CAP], start=True, stop=True
                          ).then_inc(s["ejT_ps"], 1)

            def numbers(m):
                _, vals = nc.values_load_multi_w_load_instructions(
                    etab[0:1, bass.ds(at(m) * CH, CH)], engines=(mybir.EngineType.PE,), min_val=0, max_val=NE - 1)
                return vals

            def turn_rows(m, k, arrived):
                pe.wait_ge(xg_in[k], arrived)
                if not isinstance(m[0], int) or m[1] >= 2:
                    pe.wait_ge(s["g_xT_sb"], at(m, -1))
                for j in range(CH):
                    ins = t_.transpose(psA[0][:, k % 2, j * P:(j + 1) * P], xg[k][:, j, :], ident[:])
                ins.then_inc(s["g_xT_ps"], 1)

            def times_keys(m, k, es):
                pe.wait_ge(s["g_xT_sb"], at(m, 1))
                if not isinstance(m[0], int) or m[1] >= 2:
                    pe.wait_ge(s["g_h_sb"], at(m, -1))
                for j in range(CH):
                    ins = t_.matmul(psA[1][:, k, j * P:(j + 1) * P], xT[k][:, j * P:(j + 1) * P],
                                    keys_sb[:, bass.ds(es[j], 1), :].rearrange("p a d -> p (a d)"), start=True, stop=True)
                ins.then_inc(s["g_h_ps"], 1)

            def turn_hidden(m, k):
                pe.wait_ge(s["g_h_sb"], at(m, 1))
                if not isinstance(m[0], int) or m[1] >= 2:
                    pe.wait_ge(s["g_hT_sb"], at(m, -1))
                for j in range(CH):
                    ins = t_.transpose(psB[k][:, j * P:(j + 1) * P], hr[k][:, j * P:(j + 1) * P], ident[:])
                ins.then_inc(s["g_hT_ps"], 1)

            def times_values(m, k, es):
                pe.wait_ge(s["g_hT_sb"], at(m, 1))
                if not isinstance(m[0], int) or m[1] >= 2:
                    pe.wait_ge(s["g_y_sb"], at(m, -1))
                for j in range(CH):
                    ins = t_.matmul((psO, psM)[k][:, j * D:(j + 1) * D], hT[k][:, j * P:(j + 1) * P],
                                    vals_sb[:, bass.ds(es[j], 1), :].rearrange("p a d -> p (a d)"), start=True, stop=True)
                ins.then_inc(s["g_y_ps"], 1)

            pe.wait_ge(s["etab_done"], GROUPS)
            pe.wait_ge(k_in, 16)
            pe.wait_ge(v_in, 16)
            turn_rows((0, 0), 0, 16)
            turn_rows((0, 1), 1, 16)
            times_keys((0, 0), 0, numbers((0, 0)))
            turn_hidden((0, 0), 0)

            def step(m, arrived):
                base, off = m
                turn_rows((base, off + 1), (off + 1) % UN, arrived)
                times_keys(m, off % 2, numbers(m))
                times_values((base, off - 1), (off - 1) % 2, numbers((base, off - 1)))
                turn_hidden(m, off % 2)

            for m in range(1, UN):
                step((0, m), 16 * ((m + 1) // UN + 1))
            with pe.Fori(1, NCH // UN - 1) as r:
                for u in range(UN):
                    step((r * UN, u), r * 16 + 16 * ((u + 1) // UN + 1))
            for m in range(NCH - UN, NCH - 1):
                step((0, m), 16 * ((m + 1) // UN + 1))
            m = (0, NCH - 1)
            times_keys(m, (NCH - 1) % 2, numbers(m))
            times_values((0, NCH - 2), (NCH - 2) % 2, numbers((0, NCH - 2)))
            turn_hidden(m, (NCH - 1) % 2)
            times_values(m, (NCH - 1) % 2, numbers(m))


_INS = ["x", "ctx_1024", "condB_tau", "fside_BxS2_0", "L0_xcond_Wq", "L0_xcond_bq", "L0_xcond_Wk", "L0_xcond_bk",
        "L0_xcond_Wv", "L0_xcond_bv", "L0_xcond_Wo", "L0_xcond_bo", "L0_ffn_expert_sel", "L0_ffn_keys", "L0_ffn_values"]


def kernel(**inputs):
    import numpy as _np
    import concourse.bacc as _bacc
    from concourse import mybir as _mybir
    from concourse.bass_utils import run_bass_kernel_spmd as _run

    nc = _bacc.Bacc("TRN2", target_bir_lowering=False, num_devices=1)
    arrays, args = {}, []
    for name in _INS:
        a = _np.ascontiguousarray(inputs[name])
        arrays[f"in_{name}_dram"] = a
        args.append(nc.dram_tensor(f"in_{name}_dram", a.shape, _mybir.dt.from_np(a.dtype), kind="ExternalInput").ap())
    args.append(nc.dram_tensor("out_0_dram", (B, L, D), F32, kind="ExternalOutput").ap())
    for name in ("sorted_rows", "result_rows"):
        args.append(nc.dram_tensor(name, (GROUPS * CAP * P, D), F32, kind="Internal").ap())
    block_kernel(nc, *args)
    r = _run(nc, [arrays], core_ids=[0])
    return r.results[0]["out_0_dram"]
```

```python
from contextlib import ExitStack

import concourse.bass as bass
from concourse import mybir

F32 = mybir.dt.float32
BF16 = mybir.dt.bfloat16
F32R = mybir.dt.float32r
I32 = mybir.dt.int32
U32 = mybir.dt.uint32
ALU = mybir.AluOpType
ACT = mybir.ActivationFunctionType
AX = mybir.AxisListType

P = 128
B, L, D = 4, 512, 128
S = 77
H, E = 16, 8
HG = 4
NG = H // HG
R = HG * S
TR = R - 2 * P
RP = 2 * P + P // 2
NU = NG * 2 + NG // 2
HR = HG * E
T = L // P
NT = B * T
NE, TOPK = 64, 4
GROUPS = 2
BG = B // GROUPS
TG = T * BG
CAP = TG * TOPK + NE
CH = 4
NCH = GROUPS * CAP // CH
UN = 4
SCALE = 1.0 / float(E) ** 0.5
EPS = 1e-5
ZW = 4


def block_kernel(nc, x, ctx_in, tau, fside, Wq, bq, Wk, bk, Wv, bv, Wo, bo, esel, keys, values, out, xs, ys):
    xf = x.rearrange("b l d -> (b l) d")
    of = out.rearrange("b l d -> (b l) d")

    with ExitStack() as stack:
        def sb(name, shape, dt=F32):
            return stack.enter_context(nc.sbuf_tensor(name, shape, dt))

        def sem(name):
            return stack.enter_context(nc.semaphore(name))

        x_sb = sb("x_sb", [P, NT, D])
        x1_sb = x_sb
        xn2_sb = sb("xn2_sb", [P, NT, D])
        keys_sb = sb("keys_sb", [P, NE, P])
        vals_sb = sb("vals_sb", [P, NE, D])
        wT = sb("wT", [P, 4, D])
        selT = sb("selT", [P, NE])
        bq_col = sb("bq_col", [P, 1])
        bkS = sb("bkS", [3 * HR, NG])
        bv_bc = sb("bv_bc", [P, D])
        bo_bc = sb("bo_bc", [P, D])
        tau_bc = sb("tau_bc", [P, B])
        K3 = sb("K3", [P, NG, B, S], F32R)
        vt = sb("vt", [P, B, 3, D])
        Vb = sb("Vb", [P, NU, 4, HR])

        ident = sb("ident", [P, P])
        identb = sb("identb", [P, P], BF16)
        onesf = sb("onesf", [P, P])
        onesb = sb("onesb", [P, P], BF16)
        tri = sb("tri", [P, P], BF16)
        onev = sb("onev", [P, 3, HG])
        vm0 = sb("vm0", [P, 3, HG])
        vm1 = sb("vm1", [P, HG])
        vm2 = sb("vm2", [P, HG])
        vmask = sb("vmask", [P, 4, HG])
        selq = sb("selq", [P, NG, 6, HR], F32R)
        pidx = sb("pidx", [P, 1], I32)
        pint = sb("pint", [P, 5], I32)
        pflt = sb("pflt", [P, 5])
        hrow = sb("hrow", [P, HG])
        hmask = sb("hmask", [P, HG])
        isd0 = sb("isd0", [P, 1])
        isd = sb("isd", [P, 1])
        rm = sb("rm", [P, 3])
        iota_e = sb("iota_e", [P, NE])
        jcol = sb("jcol", [P, 1])
        gbase = sb("gbase", [P, 1])
        zeros64 = sb("zeros64", [P, NE])
        mhalf = sb("mhalf", [P, T])
        zero = sb("zero", [P, ZW * D])

        st1 = sb("st1", [P, T, 6])
        mv1 = sb("mv1", [P, T, 2])
        ve1 = sb("ve1", [P, T])
        rs1 = sb("rs1", [P, T])
        xn1 = sb("xn1", [P, T, D])
        xnT = sb("xnT", [P, L])
        qf = xnT
        qh = sb("qh", [P, L], F32R)
        ql = sb("ql", [P, L], F32R)
        qs = [sb(f"qs{k}", [P, NG, L], F32R) for k in range(BG)]
        Ks = [sb(f"Ks{k}", [P, NG, R], F32R) for k in range(BG)]
        KsT = [sb(f"KsT{k}", [P, NG, P], F32R) for k in range(BG)]
        mx = [sb(f"mx{k}", [P, T, H]) for k in range(BG)]
        negm = sb("negm", [P, T * NG, HR], BF16)
        PT = [sb(f"PT{k}", [P, NU, L]) for k in range(BG)]
        rden = sb("rden", [2 * HR, L])
        aT = sb("aT", [P, L])
        st2 = sb("st2", [P, T, 6])
        mv2 = sb("mv2", [P, T, 2])
        ve2 = sb("ve2", [P, T])
        rs2 = sb("rs2", [P, T])
        xn2T = sb("xn2T", [P, L])

        ex = sb("ex", [P, T, NE])
        wv = sb("wv", [P, T, NE])
        top = sb("top", [P, T, 8])
        tidx = sb("tidx", [P, T, 8], U32)
        tidf = sb("tidf", [P, T, 8])
        rgate = sb("rgate", [P, T, TOPK])
        gates = sb("gates", [P, NT * TOPK])
        OH = sb("OH", [P, TG, TOPK, NE])
        ctxT = OH[:].rearrange("p t k e -> p (t k e)")[:, 0:B * RP].rearrange("p (b r) -> p b r", b=B)
        mask = sb("mask", [P, TG, NE], BF16)
        cnt_i = sb("cnt_i", [P, NE], I32)
        cnt_t = sb("cnt_t", [P, NE], I32)
        ntile = sb("ntile", [P, NE])
        incl = sb("incl", [P, NE])
        excl = sb("excl", [P, NE])
        sbase = sb("sbase", [P, NE])
        pos = xnT[:].rearrange("p (t e) -> p t e", e=NE)
        slotf = sb("slotf", [P, TG * TOPK])
        slots = sb("slots", [P, NT * TOPK], I32)
        lecmp = sb("lecmp", [P, NE])
        ej = sb("ej", [P, 1])
        etab = sb("etab", [1, GROUPS * CAP], I32)

        pt0 = PT[0][:].rearrange("p v l -> p (v l)")
        pt1 = PT[1][:].rearrange("p v l -> p (v l)")
        o = 0
        w_nat = pt1[:, o:o + 4 * D].rearrange("p (j d) -> p j d", d=D)
        o += 4 * D
        ctx_nat = pt1[0:S, o:o + B * D].rearrange("p (b d) -> p b d", b=B)
        o += B * D
        sel_nat = pt1[0:NE, o:o + D]
        o += D
        KTf = pt1[:, o:o + NG * B * S].rearrange("p (g r) -> p g r", g=NG)
        o += NG * B * S
        tau_rep, delta_bc, dl, d3 = [pt1[:, o + j * B * S:o + (j + 1) * B * S] for j in range(4)]
        wkS = pt1[:, o + 5 * B * S:o + 5 * B * S + NG * 3 * HR].rearrange("p (g r c) -> p g r c", g=NG, r=3)
        dh = pt1[:, o + 4 * B * S:o + 5 * B * S].bitcast(F32R)
        gb = pt0[:, 0:TG * TOPK * D].rearrange("p (j d) -> p j d", d=D)
        room = [pt1[:, j * CH * P:(j + 1) * CH * P] for j in range(NU)] + [pt0[:, j * CH * P:(j + 1) * CH * P] for j in range(NU - 2, NU)]
        xg = [room[k].rearrange("p (a d) -> p a d", a=CH) for k in range(UN)]
        xT, hr, hT, yb = room[4:6], room[6:8], room[8:10], room[10:12]
        ot = [xn1[:, k, :] for k in range(2)]

        psA = stack.enter_context(nc.psum_tensor("psA", [P, NG, 512], F32))
        psB = [stack.enter_context(nc.psum_tensor(f"psB{k}", [P, 512], F32)) for k in range(2)]
        psO = stack.enter_context(nc.psum_tensor("psO", [P, 512], F32))
        psM = stack.enter_context(nc.psum_tensor("psM", [P, 512], F32))
        mTp = psO[:, 0:256].bitcast(BF16)

        x0_in, x_in, w_in, k_in, v_in = sem("x0_in"), sem("x_in"), sem("w_in"), sem("k_in"), sem("v_in")
        zeroed = [sem(f"zeroed{g}") for g in range(GROUPS)]
        scattered = [sem(f"scattered{g}") for g in range(GROUPS)]
        ones_set = sem("ones_set")
        zero_set = sem("zero_set")
        ctxT_zeroed = sem("ctxT_zeroed")
        kb_zeroed = sem("kb_zeroed")
        negm_zeroed = sem("negm_zeroed")
        ident_set = sem("ident_set")
        identb_set = sem("identb_set")
        tri_set = sem("tri_set")
        small_set = sem("small_set")
        vm0_set = sem("vm0_set")
        vmask_set = sem("vmask_set")
        pint_set = sem("pint_set")
        pflt_set = sem("pflt_set")
        hrow_set = sem("hrow_set")
        hmask_set = sem("hmask_set")
        rm_set = sem("rm_set")
        iota_set = sem("iota_set")
        wT_ps = sem("wT_ps")
        wT_sb = sem("wT_sb")
        ctxT_ps = sem("ctxT_ps")
        ctxT_sb = sem("ctxT_sb")
        selT_ps = sem("selT_ps")
        selT_sb = sem("selT_sb")
        wkS_set = sem("wkS_set")
        isd_set = sem("isd_set")
        tau_set = sem("tau_set")
        dh_set = sem("dh_set")
        dl_set = sem("dl_set")
        d3_set = sem("d3_set")
        kT_ps = sem("kT_ps")
        kTf_set = sem("kTf_set")
        k3h_set = sem("k3h_set")
        k3_set = sem("k3_set")
        delta_set = sem("delta_set")
        v_ps = sem("v_ps")
        vt_sb = sem("vt_sb")
        vb_set = sem("vb_set")
        den_set = sem("den_set")
        xb_ready = sem("xb_ready")
        ln1_stats = sem("ln1_stats")
        ln1_aggr = sem("ln1_aggr")
        ln1_rstd = sem("ln1_rstd")
        xn1_ready = sem("xn1_ready")
        xnT_ps = sem("xnT_ps")
        xnT_sb = sem("xnT_sb")
        q_ps = sem("q_ps")
        qh_sb = sem("qh_sb")
        qf_sb = sem("qf_sb")
        stack_ps = sem("stack_ps")
        stack_sb = sem("stack_sb")
        rden_done = sem("rden_done")
        isd0_set = sem("isd0_set")
        selq_zeroed = sem("selq_zeroed")
        selq_set = sem("selq_set")
        vb_zeroed = sem("vb_zeroed")
        vm1_set = sem("vm1_set")
        vm2_set = sem("vm2_set")
        ql_sb = sem("ql_sb")
        kb_ready = sem("kb_ready")
        mT_act = sem("mT_act")
        mT_dve = sem("mT_dve")
        ve_done = sem("ve_done")
        ve2_done = sem("ve2_done")
        a_ps = sem("a_ps")
        max_done = sem("max_done")
        split_hi = sem("split_hi")
        split_lo = sem("split_lo")
        mT_ps = sem("mT_ps")
        b_ps = sem("b_ps")
        exp_done = sem("exp_done")
        o_ps = sem("o_ps")
        att_done = sem("att_done")
        y_ps = sem("y_ps")
        x1_done = sem("x1_done")
        ln2_stats = sem("ln2_stats")
        ln2_aggr = sem("ln2_aggr")
        ln2_rstd = sem("ln2_rstd")
        xn2_done = sem("xn2_done")
        xn2T_ps = sem("xn2T_ps")
        xn2T_sb = sem("xn2T_sb")
        lg_ps = sem("lg_ps")
        ex_done = sem("ex_done")
        w_done = sem("w_done")
        top_done = sem("top_done")
        idx_done = sem("idx_done")
        tidf_done = sem("tidf_done")
        rgate_done = sem("rgate_done")
        gates_done = sem("gates_done")
        oh_done = sem("oh_done")
        mask_done = sem("mask_done")
        route_ps = sem("route_ps")
        cnt_done = sem("cnt_done")
        shift_done = sem("shift_done")
        ntile_done = sem("ntile_done")
        incl_done = sem("incl_done")
        excl_done = sem("excl_done")
        base_done = sem("base_done")
        pos_done = sem("pos_done")
        prod_done = sem("prod_done")
        slotf_done = sem("slotf_done")
        slots_done = sem("slots_done")
        ej_done = sem("ej_done")
        ejT_ps = sem("ejT_ps")
        etab_done = sem("etab_done")
        step_done = sem("step_done")
        g_xT_ps = sem("g_xT_ps")
        g_xT_sb = sem("g_xT_sb")
        g_h_ps = sem("g_h_ps")
        g_h_sb = sem("g_h_sb")
        g_hT_ps = sem("g_hT_ps")
        g_hT_sb = sem("g_hT_sb")
        g_y_ps = sem("g_y_ps")
        g_y_sb = sem("g_y_sb")
        acc_done = sem("acc_done")
        xg_in = [sem(f"xg_in{k}") for k in range(UN)]
        y_out = [sem(f"y_out{k}") for k in range(2)]
        gb_in = [sem(f"gb_in{k}") for k in range(TG)]
        o_out = [sem(f"o_out{k}") for k in range(2)]
        NSMALL = 14

        def at(m, d=0):
            return m[0] + (m[1] + d)

        block = stack.enter_context(nc.Block())

        def load_rows(sp, m, k):
            sp.dma_start(xg[k], xs[bass.ds(at(m) * (CH * P), CH * P), :].rearrange("(a p) d -> p a d", p=P)
                         ).then_inc(xg_in[k], 16)

        def store_rows(sp, m, k):
            sp.wait_ge(g_y_sb, at(m, 1))
            sp.dma_start(ys[bass.ds(at(m) * (CH * P), CH * P), :].rearrange("(a p) d -> p a d", p=P),
                         yb[k].rearrange("p (a d) -> p a d", a=CH)).then_inc(y_out[k], 16)

        @block.sync
        def _(sp):
            xv = xf.rearrange("(t p) d -> p t d", p=P)
            sp.dma_start(x_sb[:, 0:T], xv[:, 0:T]).then_inc(x0_in, 16)
            for j, w in enumerate((Wq, Wk, Wv, Wo)):
                sp.dma_start(w_nat[:, j], w).then_inc(w_in, 16)
            sp.dma_start(ctx_nat, ctx_in.rearrange("b s d -> s b d")).then_inc(w_in, 16)
            sp.dma_start(x_sb[:, T:NT], xv[:, T:NT]).then_inc(x_in, 16)
            sp.wait_ge(zero_set, 1)
            zr = P * ZW
            half = GROUPS * CAP * P // GROUPS // zr
            for j in range(half):
                sp.dma_start(xs[j * zr:(j + 1) * zr, :].rearrange("(p r) d -> p (r d)", p=P), zero[:]).then_inc(zeroed[0], 16)
            sp.dma_start(keys_sb[:], keys.rearrange("e d k -> d e k")).then_inc(k_in, 16)
            sp.dma_start(vals_sb[:], values.rearrange("e k v -> k e v")).then_inc(v_in, 16)
            for j in range(half, GROUPS * half):
                sp.dma_start(xs[j * zr:(j + 1) * zr, :].rearrange("(p r) d -> p (r d)", p=P), zero[:]).then_inc(zeroed[1], 16)
            per = NCH // GROUPS
            sp.wait_ge(o_ps, 2 * B)
            for g in range(GROUPS):
                sp.wait_ge(scattered[g], 16 * TG * TOPK)
                if g == 0:
                    for k in range(UN):
                        load_rows(sp, (0, k), k)
                    lo = 0
                else:
                    for k in range(UN):
                        m = g * per - UN + k
                        sp.wait_ge(g_xT_ps, m + 1)
                        load_rows(sp, (0, m + UN), k)
                        store_rows(sp, (0, m), k % 2)
                    lo = g * per
                hi = (g + 1) * per - UN
                with sp.Fori(lo // UN, hi // UN) as r:
                    for k in range(UN):
                        sp.wait_ge(g_xT_ps, r * UN + (k + 1))
                        load_rows(sp, (r * UN, k + UN), k)
                        store_rows(sp, (r * UN, k), k % 2)
            for k in range(UN):
                store_rows(sp, (0, NCH - UN + k), k % 2)
            with sp.Fori(0, NT // 2) as r:
                t0 = r * 2
                for k in range(2):
                    sp.wait_ge(acc_done, t0 * TOPK + (k + 1) * TOPK)
                    sp.dma_start(of[bass.ds((t0 + k) * P, P), :], ot[k]).then_inc(o_out[k], 16)
            for k in range(2):
                sp.wait_ge(o_out[k], 16 * NT // 2)

        @block.gpsimd
        def _(pool):
            g = nc.gpsimd
            g.memset(onesf[:], 1.0).then_inc(ones_set, 1)
            g.memset(onev[:], 1.0).then_inc(ones_set, 1)
            g.memset(onesb[:], 1.0).then_inc(ones_set, 1)
            g.iota(pidx[:], pattern=[[0, 1]], base=0, channel_multiplier=1).then_inc(iota_set, 1)
            g.iota(iota_e[:], pattern=[[1, NE]], base=0, channel_multiplier=0,
                   allow_small_or_imprecise_dtypes=True).then_inc(iota_set, 1)
            g.iota(jcol[:], pattern=[[0, 1]], base=0, channel_multiplier=1,
                   allow_small_or_imprecise_dtypes=True).then_inc(iota_set, 1)
            g.iota(hrow[:], pattern=[[1, HG]], base=0, channel_multiplier=0,
                   allow_small_or_imprecise_dtypes=True).then_inc(iota_set, 1)
            g.memset(mhalf[:], -0.5).then_inc(small_set, 1)
            pool.wait_ge(ones_set, 3)
            g.affine_select(out=ident[:], in_=onesf[:], pattern=[[-1, P]], compare_op=ALU.is_equal, fill=0.0,
                            base=0, channel_multiplier=1).then_inc(ident_set, 1)
            g.memset(ctxT[:, :, R:RP], 0.0).then_inc(ctxT_zeroed, 1)
            g.affine_select(out=identb[:], in_=onesb[:], pattern=[[-1, P]], compare_op=ALU.is_equal, fill=0.0,
                            base=0, channel_multiplier=1).then_inc(identb_set, 1)
            g.affine_select(out=vm0[:], in_=onev[:], pattern=[[P, 3], [-S, HG]], compare_op=ALU.is_ge, fill=0.0,
                            base=0, channel_multiplier=1).then_inc(vm0_set, 1)
            g.affine_select(out=vm1[:], in_=onev[:, 0, :], pattern=[[-S, HG]], compare_op=ALU.is_ge, fill=0.0,
                            base=P + P // 2, channel_multiplier=1).then_inc(vm1_set, 1)
            pool.wait_ge(vm0_set, 1)
            g.affine_select(out=vmask[:, 0:3], in_=vm0[:], pattern=[[-P, 3], [S, HG]], compare_op=ALU.is_ge, fill=0.0,
                            base=S - 1, channel_multiplier=-1).then_inc(vmask_set, 1)
            pool.wait_ge(vm1_set, 1)
            g.affine_select(out=vm2[:], in_=vm1[:], pattern=[[S, HG]], compare_op=ALU.is_ge, fill=0.0,
                            base=S - 1 - P - P // 2, channel_multiplier=-1).then_inc(vm2_set, 1)
            pool.wait_ge(vm2_set, 1)
            g.affine_select(out=vmask[:, 3], in_=vm2[:], pattern=[[0, HG]], compare_op=ALU.is_ge, fill=0.0,
                            base=-(P // 2), channel_multiplier=1).then_inc(vmask_set, 1)
            g.memset(selq[:].bitcast(F32), 0.0).then_inc(selq_zeroed, 1)
            g.memset(Vb[:], 0.0).then_inc(vb_zeroed, 1)
            pool.wait_ge(ident_set, 1)
            pool.wait_ge(selq_zeroed, 1)
            eye = ident[:].rearrange("p (g c) -> p g () c", g=NG)
            g.tensor_copy(selq[:, :, 0:2, :], eye.broadcast_to([P, NG, 2, HR])).then_inc(selq_set, 1)
            g.tensor_copy(selq[:, :, 4:5, :], eye).then_inc(selq_set, 1)
            for k in range(BG):
                g.memset(KsT[k][:].bitcast(F32), 0.0).then_inc(kb_zeroed, 1)
            g.memset(negm[:], 0.0).then_inc(negm_zeroed, 1)
            pool.wait_ge(negm_zeroed, 1)
            g.memset(negm[:, :, 2 * HG:2 * HG + 2], 1.0).then_inc(negm_zeroed, 1)
            g.affine_select(out=tri[:], in_=onesb[:], pattern=[[1, P]], compare_op=ALU.is_gt, fill=0.0,
                            base=0, channel_multiplier=-1).then_inc(tri_set, 1)
            g.memset(zeros64[:], 0.0).then_inc(small_set, 1)
            g.memset(gbase[:], 0.0).then_inc(small_set, 1)
            pool.wait_ge(vmask_set, 2)
            pool.wait_ge(vb_zeroed, 1)
            for p in range(NG // 2):
                for a in range(2):
                    v0, tail = 5 * p + 2 * a, 5 * p + 4
                    g.tensor_copy(Vb[:, v0:v0 + 2, 2 + a, :].rearrange("p c (h e) -> p c h e", h=HG),
                                  vmask[:, 0:2, :].rearrange("p c h -> p c h ()").broadcast_to([P, 2, HG, E])
                                  ).then_inc(den_set, 1)
                    g.tensor_copy(Vb[:, tail:tail + 1, 2 + a, :].rearrange("p c (h e) -> p c h e", h=HG),
                                  vmask[:, 2 + a:3 + a, :].rearrange("p c h -> p c h ()").broadcast_to([P, 1, HG, E])
                                  ).then_inc(den_set, 1)

            def spread_keys(n, k):
                pool.wait_ge(k3_set, 1)
                pool.wait_ge(delta_set, 1)
                pool.wait_ge(hmask_set, 2)
                if n >= BG:
                    pool.wait_ge(b_ps, NU * (n - BG + 1))
                for gi in range(NG):
                    g.tensor_tensor(Ks[k][:, gi, 0:R].rearrange("p (h s) -> p h s", h=HG),
                                    K3[:, gi, n:n + 1, :].bitcast(F32).broadcast_to([P, HG, S]),
                                    hmask[:].rearrange("p h -> p h ()").broadcast_to([P, HG, S]), ALU.mult)
                for a in range(2):
                    ins = g.tensor_tensor(KsT[k][:].rearrange("p (b a) c -> p a b c", a=2)[:, a, :, 64 * a:64 * a + TR],
                                          K3[:].rearrange("p (b a) n s -> p a b n s", a=2)[:, a, :, n, S - TR:S].bitcast(F32),
                                          hmask[:, HG - 1:HG].rearrange("p h -> p h ()").broadcast_to([P, NG // 2, TR]),
                                          ALU.mult)
                ins.then_inc(kb_ready, 1)

            def rstd(n, ve, rs, eps, done):
                pool.wait_ge(eps, n + 1)
                g.tensor_tensor(rs[:], ve[:], mhalf[:], ALU.pow).then_inc(done, 1)

            def add_bo(n):
                pool.wait_ge(xn1_ready, n + 1)
                pool.wait_ge(w_in, 16 * NSMALL)
                g.tensor_tensor(x_sb[:, n * T:(n + 1) * T, :], x_sb[:, n * T:(n + 1) * T, :],
                                bo_bc[:].rearrange("p d -> p () d").broadcast_to([P, T, D]), ALU.add
                                ).then_inc(xb_ready, 1)

            scatters = []

            def scatter(count):
                for _ in range(min(count, len(scatters))):
                    j = scatters.pop(0)
                    g.indirect_dma_start(out=xs[:, :], out_offset=bass.IndirectOffsetOnAxis(ap=slots[:, j:j + 1], axis=0),
                                         in_=xn2_sb[:, j // TOPK, :], in_offset=None).then_inc(scattered[j // (TG * TOPK)], 16)

            def spread_values(b):
                pool.wait_ge(vt_sb, b + 1)
                if b:
                    pool.wait_ge(o_ps, 2 * b)
                for p in range(NG // 2):
                    for a in range(2):
                        cols = slice((2 * p + a) * HR, (2 * p + a + 1) * HR)
                        v0, tail = 5 * p + 2 * a, 5 * p + 4
                        g.tensor_tensor(Vb[:, v0:v0 + 2, a, :].rearrange("p c (h e) -> p c h e", h=HG),
                                        vt[:, b, 0:2, cols].rearrange("p c (h e) -> p c h e", h=HG),
                                        vmask[:, 0:2, :].rearrange("p c h -> p c h ()").broadcast_to([P, 2, HG, E]),
                                        ALU.mult)
                        ins = g.tensor_tensor(Vb[:, tail:tail + 1, a, :].rearrange("p c (h e) -> p c h e", h=HG),
                                              vt[:, b, 2:3, cols].rearrange("p c (h e) -> p c h e", h=HG),
                                              vmask[:, 2 + a:3 + a, :].rearrange("p c h -> p c h ()"
                                                                                 ).broadcast_to([P, 1, HG, E]), ALU.mult)
                ins.then_inc(vb_set, 1)

            pool.wait_ge(small_set, 1)
            rstd(0, ve1, rs1, ve_done, ln1_rstd)
            spread_keys(0, 0)
            add_bo(0)
            rstd(1, ve1, rs1, ve_done, ln1_rstd)
            spread_values(0)
            spread_keys(1, 1)
            add_bo(1)
            for n in range(B + 2):
                if BG <= n + 1 < B:
                    spread_keys(n + 1, (n + 1) % 2)
                scatter(12)
                if 2 <= n <= B:
                    spread_values(n - 1)
                if n + 2 < B:
                    rstd(n + 2, ve1, rs1, ve_done, ln1_rstd)
                if 1 <= n <= B:
                    rstd(n - 1, ve2, rs2, ve2_done, ln2_rstd)
                if n + 2 < B:
                    add_bo(n + 2)
                if n >= BG + 1 and (n - 1) % BG == 0:
                    i = (n - 1) // BG - 1
                    pool.wait_ge(slots_done, i + 1)
                    pool.wait_ge(xn2_done, BG * (i + 1))
                    pool.wait_ge(zeroed[i], 16 * CAP // ZW)
                    scatters += [i * TG * TOPK + j for j in range(TG * TOPK)]
            scatter(len(scatters))

            for j in range(NT * TOPK):
                if j % (TG * TOPK) == 0:
                    grp = j // (TG * TOPK)
                    for k in range(2):
                        pool.wait_ge(y_out[k], 16 * NCH // 2 // GROUPS * (grp + 1))
                if j >= TG * TOPK:
                    pool.wait_ge(acc_done, j - TG * TOPK + 1)
                g.indirect_dma_start(out=gb[:, j % (TG * TOPK), :], out_offset=None, in_=ys[0:(grp + 1) * CAP * P, :],
                                     in_offset=bass.IndirectOffsetOnAxis(ap=slots[:, j:j + 1], axis=0)
                                     ).then_inc(gb_in[j // TOPK % TG], 16)

        @block.scalar
        def _(act):
            a = nc.scalar
            with nc.allow_non_contiguous_dma(reason="bias columns and broadcast rows, small"):
                act.dma_start(sel_nat, esel).then_inc(w_in, 16)
                act.dma_start(bq_col[:], bq.rearrange("(p a) -> p a", a=1)).then_inc(w_in, 16)
                for r in range(3):
                    act.dma_start(bkS[r * HR:(r + 1) * HR, :], bk.rearrange("(g p) -> p g", p=HR)).then_inc(w_in, 16)
                act.dma_start(bv_bc[:], bv.rearrange("(a d) -> a d", a=1).broadcast_to([P, D])).then_inc(w_in, 16)
                act.dma_start(bo_bc[:], bo.rearrange("(a d) -> a d", a=1).broadcast_to([P, D])).then_inc(w_in, 16)
                act.dma_start(tau_bc[:], tau.rearrange("(a d) -> a d", a=1).broadcast_to([P, B])).then_inc(w_in, 16)
                act.dma_start(delta_bc.rearrange("p (b s) -> p b s", b=B),
                              fside.rearrange("(a b) s -> a b s", a=1).broadcast_to([P, B, S])).then_inc(w_in, 16)
            act.wait_ge(wT_ps, 1)
            a.copy(wkS, psB[0][:, D:2 * D].rearrange("p (g c) -> p g () c", g=NG).broadcast_to([P, NG, 3, HR])
                   ).then_inc(wkS_set, 1)
            a.copy(wT[:].rearrange("p j d -> p (j d)"), psB[0][:]).then_inc(wT_sb, 1)

            def copy_xnT(n):
                act.wait_ge(xnT_ps, n + 1)
                if n:
                    act.wait_ge(ql_sb, n)
                a.copy(xnT[:], psA[:, NG - 1, :]).then_inc(xnT_sb, 1)

            def copy_q(n):
                act.wait_ge(q_ps, n + 1)
                if n:
                    act.wait_ge(stack_ps, NG * n)
                a.activation(qh[:], psA[:, 2, :], ACT.Identity, bias=bq_col[:, 0:1]).then_inc(qh_sb, 1)
                a.activation(qf[:], psA[:, 2, :], ACT.Identity, bias=bq_col[:, 0:1]).then_inc(qf_sb, 1)

            def copy_stack(n, k):
                act.wait_ge(isd0_set, 2)
                for gi in range(NG):
                    act.wait_ge(stack_ps, NG * n + gi + 1)
                    a.activation(qs[k][:, gi, :], psA[:, gi, :], ACT.Identity, bias=isd0[:, 0:1]).then_inc(stack_sb, 1)

            def copy_shifts(n, k):
                act.wait_ge(mT_ps, n + 1)
                for gi in range(2):
                    a.copy(qs[k][3 * HR:P, gi, :], mTp[gi * HR:(gi + 1) * HR, :]).then_inc(mT_act, 1)

            def exps(n, k, v0, v1):
                for v in range(v0, v1):
                    act.wait_ge(b_ps, NU * n + v + 1)
                    a.activation(PT[k][:, v, :], psB[v % 2][:], ACT.Exp, scale=SCALE).then_inc(exp_done, 1)

            def copy_xn2T(n, k):
                act.wait_ge(xn2T_ps, n + 1)
                a.copy(xn2T[:], psM[:]).then_inc(xn2T_sb, 1)

            def exp_logits(n, k):
                act.wait_ge(lg_ps, n + 1)
                if n:
                    act.wait_ge(w_done, n)
                a.activation(ex[:].rearrange("p t e -> p (t e)"), psM[:, 0:T * NE], ACT.Exp,
                             scale=-1.0).then_inc(ex_done, 1)

            act.wait_ge(kTf_set, NG)
            a.copy(K3[0:3 * HR].rearrange("p g b s -> p g (b s)"), KTf[0:3 * HR]).then_inc(k3h_set, 1)
            copy_xnT(0)
            copy_q(0)
            copy_stack(0, 0)
            for n in range(B + 2):
                k = n % 2
                more = n + 1 < B
                if more:
                    copy_xnT(n + 1)
                if n < B:
                    copy_shifts(n, k)
                if n >= 2:
                    copy_xn2T(n - 2, 0)
                if more:
                    copy_q(n + 1)
                if n >= 2:
                    exp_logits(n - 2, 0)
                if n < B:
                    exps(n, k, 0, 3)
                if more:
                    copy_stack(n + 1, 1 - k)
                if n < B:
                    exps(n, k, 3, NU)

            def copy_gxT(m, k):
                act.wait_ge(g_xT_ps, at(m, 1))
                a.copy(xT[k], psA[:, k, :]).then_inc(g_xT_sb, 1)

            def copy_ghT(m, k):
                act.wait_ge(g_hT_ps, at(m, 1))
                a.copy(hT[k], psB[k][:]).then_inc(g_hT_sb, 1)

            copy_gxT((0, 0), 0)
            copy_gxT((0, 1), 1)
            copy_ghT((0, 0), 0)
            with act.Fori(0, (NCH - 2) // 2) as r:
                for k in range(2):
                    copy_gxT((r * 2, k + 2), k)
                    copy_ghT((r * 2, k + 1), (k + 1) % 2)
            copy_ghT((0, NCH - 1), (NCH - 1) % 2)

        @block.vector
        def _(dve):
            v = nc.vector
            v.memset(zero[:], 0.0).then_inc(zero_set, 1)
            dve.wait_ge(iota_set, 4)
            v.tensor_scalar(pint[:, 0:1], pidx[:], 3, 3, ALU.logical_shift_right, ALU.bitwise_and).then_inc(pint_set, 1)
            v.tensor_scalar(pint[:, 1:2], pidx[:], 31, None, ALU.bitwise_and).then_inc(pint_set, 1)
            v.tensor_scalar(pint[:, 2:3], pidx[:], 3, None, ALU.bitwise_and).then_inc(pint_set, 1)
            v.tensor_scalar(pint[:, 3:4], pidx[:], 1, 15, ALU.logical_shift_right, ALU.bitwise_and).then_inc(pint_set, 1)
            dve.wait_ge(pint_set, 4)
            v.tensor_copy(pflt[:, 0:4], pint[:, 0:4]).then_inc(pflt_set, 1)
            dve.wait_ge(pflt_set, 1)
            v.tensor_scalar(isd[:], pflt[:, 3:4], float(HG), None, ALU.is_equal).then_inc(isd_set, 1)
            v.memset(isd0[0:3 * HR], 0.0).then_inc(isd0_set, 1)
            v.tensor_scalar(isd0[3 * HR:P], pflt[3 * HR:P, 3:4], float(HG), None, ALU.is_equal).then_inc(isd0_set, 1)
            v.tensor_scalar(rm[:, 0:1], pflt[:, 1:2], float(2 * HG), None, ALU.is_equal).then_inc(rm_set, 1)
            v.tensor_scalar(rm[:, 1:2], pflt[:, 1:2], float(2 * HG + 1), None, ALU.is_equal).then_inc(rm_set, 1)
            v.tensor_scalar(rm[:, 2:3], pflt[:, 0:1], 0.0, None, ALU.is_equal).then_inc(rm_set, 1)
            v.tensor_scalar(hmask[0:3 * HR], hrow[0:3 * HR], pflt[0:3 * HR, 0:1], None, ALU.is_equal).then_inc(hmask_set, 1)
            dve.wait_ge(isd_set, 1)
            v.tensor_scalar(hmask[3 * HR:P], hrow[3 * HR:P], pflt[3 * HR:P, 2:3], isd[3 * HR:P, 0:1], ALU.is_equal,
                            ALU.max).then_inc(hmask_set, 1)

            def ln_stats(n, src, st, stats):
                for t in range(T):
                    ins = v.bn_stats(st[:, t, :], src(n, t))
                ins.then_inc(stats, 1)

            def ln_aggr(n, st, mv, ve, stats, aggr, eps):
                dve.wait_ge(stats, n + 1)
                for t in range(T):
                    ins = v.bn_aggr(mv[:, t, :], st[:, t, :])
                ins.then_inc(aggr, 1)
                dve.wait_ge(aggr, n + 1)
                v.tensor_scalar(ve[:], mv[:, :, 1:2].rearrange("p t a -> p (t a)"), EPS, None, ALU.add).then_inc(eps, 1)

            def ln_apply(n, src, dst, mv, rs, aggr, rstd_sem, done):
                dve.wait_ge(aggr, n + 1)
                dve.wait_ge(rstd_sem, n + 1)
                for t in range(T):
                    ins = v.tensor_scalar(dst[:, t, :], src(n, t), mv[:, t, 0:1], rs[:, t:t + 1], ALU.subtract, ALU.mult)
                ins.then_inc(done, 1)

            def x_tile(n, t):
                return x_sb[:, bass.ds(n * T + t, 1), :].rearrange("p a d -> p (a d)")

            def x1_tile(n, t):
                return x1_sb[:, bass.ds(n * T + t, 1), :].rearrange("p a d -> p (a d)")

            def norm1(n):
                dve.wait_ge(x_in if n else x0_in, 16)
                ln_stats(n, x_tile, st1, ln1_stats)
                ln_aggr(n, st1, mv1, ve1, ln1_stats, ln1_aggr, ve_done)
                if n:
                    dve.wait_ge(xnT_ps, n)
                ln_apply(n, x_tile, xn1, mv1, rs1, ln1_aggr, ln1_rstd, xn1_ready)

            def low_q(n):
                dve.wait_ge(qh_sb, n + 1)
                dve.wait_ge(qf_sb, n + 1)
                if n:
                    dve.wait_ge(stack_ps, NG * n)
                v.tensor_tensor(ql[:], qf[:], qh[:].bitcast(F32), ALU.subtract).then_inc(ql_sb, 1)

            def copy_shifts(n, k):
                dve.wait_ge(mT_ps, n + 1)
                for gi in range(2, NG):
                    v.tensor_copy(qs[k][3 * HR:P, gi, :], mTp[gi * HR:(gi + 1) * HR, :]).then_inc(mT_dve, 1)

            def maxima(n, k, u0, u1):
                for u in range(u0, u1):
                    t, p = u // 2, u % 2
                    dve.wait_ge(a_ps, 2 * T * n + u + 1)
                    v.tensor_reduce(mx[k][:, t, 8 * p:8 * p + 8].rearrange("p (a h) -> p a h", a=2),
                                    psA[:, 2 * p:2 * p + 2, 0:R].rearrange("p a (h s) -> p a h s", h=HG),
                                    AX.X, ALU.max).then_inc(max_done, 1)

            def split_max(n, k):
                dve.wait_ge(max_done, 2 * T * (n + 1))
                m = mx[k][:].rearrange("p t (g h) -> p (t g) h", g=NG)
                if n:
                    dve.wait_ge(mT_ps, n)
                v.tensor_scalar(negm[:, :, 0:HG], m, -1.0, None, ALU.mult).then_inc(split_hi, 1)
                dve.wait_ge(split_hi, n + 1)
                v.scalar_tensor_tensor(out=negm[:, :, HG:2 * HG], in0=m, scalar=-1.0, in1=negm[:, :, 0:HG],
                                       op0=ALU.mult, op1=ALU.subtract).then_inc(split_lo, 1)

            def normalise(n, p):
                src = (psO, psM)[p]
                dve.wait_ge(o_ps, 2 * n + p + 1)
                if n or p:
                    dve.wait_ge(att_done, 2 * n + p)
                v.reciprocal(rden[:], src[2 * HR:P, :]).then_inc(rden_done, 1)
                dve.wait_ge(rden_done, 2 * n + p + 1)
                v.tensor_tensor(aT[2 * HR * p:2 * HR * (p + 1), :], src[0:2 * HR, :], rden[:], ALU.mult
                                ).then_inc(att_done, 1)

            def residual(n):
                dve.wait_ge(y_ps, n + 1)
                dve.wait_ge(xb_ready, n + 1)
                v.tensor_tensor(x1_sb[:, bass.ds(n * T, T), :], psM[:].rearrange("p (t d) -> p t d", t=T),
                                x_sb[:, bass.ds(n * T, T), :],
                                ALU.add).then_inc(x1_done, 1)

            def norm2(n):
                dve.wait_ge(x1_done, n + 1)
                ln_stats(n, x1_tile, st2, ln2_stats)
                ln_aggr(n, st2, mv2, ve2, ln2_stats, ln2_aggr, ve2_done)
                ln_apply(n, x1_tile, xn2_sb[:, n * T:(n + 1) * T], mv2, rs2, ln2_aggr, ln2_rstd, xn2_done)

            def choose(n):
                dve.wait_ge(ex_done, n + 1)
                v.tensor_scalar(wv[:], ex[:], -1.0, -1.0, ALU.mult, ALU.add).then_inc(w_done, 1)
                dve.wait_ge(w_done, n + 1)
                for t in range(T):
                    ins = v.max(top[:, t, :], wv[:, t, :])
                ins.then_inc(top_done, 1)
                dve.wait_ge(top_done, n + 1)
                for t in range(T):
                    ins = v.max_index(tidx[:, t, :], top[:, t, :], wv[:, t, :])
                ins.then_inc(idx_done, 1)
                v.reciprocal(rgate[:], top[:, :, 0:TOPK]).then_inc(rgate_done, 1)
                dve.wait_ge(idx_done, n + 1)
                v.tensor_copy(tidf[:], tidx[:]).then_inc(tidf_done, 1)
                dve.wait_ge(tidf_done, n + 1)
                t0 = n % BG * T
                v.tensor_tensor(OH[:, t0:t0 + T], iota_e[:].rearrange("p e -> p () () e").broadcast_to([P, T, TOPK, NE]),
                                tidf[:, :, 0:TOPK].rearrange("p t k -> p t k ()").broadcast_to([P, T, TOPK, NE]),
                                ALU.is_equal).then_inc(oh_done, 1)
                dve.wait_ge(oh_done, n + 1)
                with nc.allow_low_precision(reason="sums of 0 and 1, at most 1: exact"):
                    v.tensor_reduce(mask[:, t0:t0 + T, :], OH[:, t0:t0 + T].rearrange("p t k e -> p t e k"), AX.X,
                                    ALU.add).then_inc(mask_done, 1)
                dve.wait_ge(rgate_done, n + 1)
                v.tensor_scalar(gates[:, bass.ds(n * (T * TOPK), T * TOPK)], rgate[:].rearrange("p t k -> p (t k)"),
                                -1.0, None, ALU.mult).then_inc(gates_done, 1)

            def route(i):
                dve.wait_ge(route_ps, i + 1)
                v.tensor_scalar(cnt_i[:], psA[:, 1, 0:NE], float(P - 1), None, ALU.add).then_inc(cnt_done, 1)
                dve.wait_ge(cnt_done, i + 1)
                v.tensor_scalar(cnt_t[:], cnt_i[:], 7, None, ALU.logical_shift_right).then_inc(shift_done, 1)
                dve.wait_ge(shift_done, i + 1)
                v.tensor_copy(ntile[:], cnt_t[:]).then_inc(ntile_done, 1)
                dve.wait_ge(ntile_done, i + 1)
                v.tensor_tensor_scan(incl[:], ntile[:], zeros64[:], gbase[:, 0:1], ALU.add, ALU.add).then_inc(incl_done, 1)
                dve.wait_ge(incl_done, i + 1)
                v.tensor_tensor(excl[:], incl[:], ntile[:], ALU.subtract).then_inc(excl_done, 1)
                dve.wait_ge(excl_done, i + 1)
                v.tensor_scalar(sbase[:], excl[:], float(P), None, ALU.mult).then_inc(base_done, 1)
                dve.wait_ge(base_done, i + 1)
                v.tensor_tensor(pos, psA[:, 0, :].rearrange("p (t e) -> p t e", t=TG),
                                sbase[:].rearrange("p e -> p () e").broadcast_to([P, TG, NE]), ALU.add
                                ).then_inc(pos_done, 1)
                dve.wait_ge(pos_done, i + 1)
                v.tensor_tensor(OH[:], OH[:], pos.rearrange("p t e -> p t () e").broadcast_to([P, TG, TOPK, NE]),
                                ALU.mult).then_inc(prod_done, 1)
                dve.wait_ge(prod_done, i + 1)
                v.tensor_reduce(slotf[:], OH[:].rearrange("p t k e -> p (t k) e"), AX.X, ALU.add).then_inc(slotf_done, 1)
                dve.wait_ge(slotf_done, i + 1)
                v.tensor_copy(slots[:, bass.ds(i * (TG * TOPK), TG * TOPK)], slotf[:]).then_inc(slots_done, 1)
                v.tensor_scalar(lecmp[0:CAP, :], incl[0:CAP, :], jcol[0:CAP, 0:1], 0.0, ALU.is_le, ALU.add,
                                accum_out=ej[0:CAP, :]).then_inc(ej_done, 1)
                dve.wait_ge(ej_done, i + 1)
                v.tensor_scalar(jcol[:], jcol[:], float(CAP), None, ALU.add).then_inc(step_done, 1)
                v.tensor_scalar(gbase[:], gbase[:], float(CAP), None, ALU.add).then_inc(step_done, 1)

            def tile_experts(i):
                dve.wait_ge(ejT_ps, i + 1)
                dve.wait_ge(step_done, 2 * i + 2)
                v.tensor_scalar(etab[0:1, bass.ds(i * CAP, CAP)], psA[0:1, 2, 0:CAP], float(NE - 1), None,
                                ALU.min).then_inc(etab_done, 1)

            norm1(0)
            dve.wait_ge(w_in, 16 * NSMALL)
            dve.wait_ge(ctxT_ps, 1)
            v.tensor_copy(ctxT[:, :, 0:R].rearrange("p b (h s) -> p b h s", h=HG),
                          psM[:, 0:B * S].rearrange("p (b s) -> p b () s", b=B).broadcast_to([P, B, HG, S])
                          ).then_inc(ctxT_sb, 1)
            v.tensor_copy(tau_rep.rearrange("p (b s) -> p b s", b=B),
                          tau_bc[:].rearrange("p b -> p b ()").broadcast_to([P, B, S])).then_inc(tau_set, 1)
            dve.wait_ge(tau_set, 1)
            for gi in range(NG):
                dve.wait_ge(kT_ps, gi + 1)
                v.scalar_tensor_tensor(out=KTf[0:3 * HR, gi, :], in0=psA[0:3 * HR, gi, 0:B * S], scalar=bkS[:, gi:gi + 1],
                                       in1=tau_rep[0:3 * HR], op0=ALU.add, op1=ALU.mult).then_inc(kTf_set, 1)
            lastb = slice(3 * HR, P)
            v.tensor_copy(dh[lastb], delta_bc[lastb]).then_inc(dh_set, 1)
            dve.wait_ge(dh_set, 1)
            v.tensor_tensor(dl[lastb], delta_bc[lastb], dh[lastb].bitcast(F32), ALU.subtract).then_inc(dl_set, 1)
            dve.wait_ge(dl_set, 1)
            dve.wait_ge(rm_set, 3)
            v.tensor_scalar(d3[lastb], dl[lastb], rm[lastb, 1:2], rm[lastb, 2:3], ALU.mult, ALU.add).then_inc(d3_set, 1)
            dve.wait_ge(d3_set, 1)
            for gi in range(NG):
                ins = v.scalar_tensor_tensor(out=K3[lastb, gi].rearrange("p b s -> p (b s)"), in0=dh[lastb].bitcast(F32),
                                             scalar=rm[lastb, 0:1], in1=d3[lastb], op0=ALU.mult, op1=ALU.add)
            ins.then_inc(delta_set, 1)
            dve.wait_ge(k3h_set, 1)
            lows = slice(HR, 2 * HR)
            k3 = K3[lows].rearrange("p g b s -> p g (b s)")
            dve.wait_ge(kTf_set, NG)
            v.tensor_tensor(k3, KTf[lows], k3.bitcast(F32), ALU.subtract).then_inc(k3_set, 1)
            dve.wait_ge(selT_ps, 1)
            v.tensor_copy(selT[:], psO[:, 0:NE]).then_inc(selT_sb, 1)
            low_q(0)
            for b in range(B):
                dve.wait_ge(v_ps, b + 1)
                v.tensor_tensor(vt[:, b], psB[b % 2][:, 0:3 * D].rearrange("p (c d) -> p c d", c=3),
                                bv_bc[:].rearrange("p d -> p () d").broadcast_to([P, 3, D]), ALU.add
                                ).then_inc(vt_sb, 1)

            norm1(1)
            dve.wait_ge(negm_zeroed, 2)
            maxima(0, 0, 0, 2 * T)
            split_max(0, 0)
            for n in range(B + 2):
                k = n % 2
                more = n + 1 < B
                if n < B:
                    copy_shifts(n, k)
                if more:
                    low_q(n + 1)
                if n >= 2:
                    choose(n - 2)
                if n >= BG + 1 and (n - 1) % BG == 0:
                    route((n - 1) // BG - 1)
                    tile_experts((n - 1) // BG - 1)
                if more:
                    maxima(n + 1, 1 - k, 0, T)
                if 1 <= n <= B:
                    normalise(n - 1, 0)
                if more:
                    maxima(n + 1, 1 - k, T, 2 * T)
                if more:
                    split_max(n + 1, 1 - k)
                if n + 2 < B:
                    norm1(n + 2)
                if 1 <= n <= B:
                    normalise(n - 1, 1)
                    residual(n - 1)
                    norm2(n - 1)

            def relu_hidden(m, k):
                dve.wait_ge(g_h_ps, at(m, 1))
                v.tensor_scalar(hr[k], psA[:, 2 + k, :], 0.0, None, ALU.max).then_inc(g_h_sb, 1)

            def copy_out(m, k, stored):
                dve.wait_ge(g_y_ps, at(m, 1))
                if stored is not None:
                    dve.wait_ge(y_out[k], stored)
                v.tensor_copy(yb[k], (psO, psM)[k][:]).then_inc(g_y_sb, 1)

            relu_hidden((0, 0), 0)
            relu_hidden((0, 1), 1)
            copy_out((0, 0), 0, None)
            relu_hidden((0, 2), 0)
            copy_out((0, 1), 1, None)
            with dve.Fori(1, (NCH - 2) // 2) as r:
                for k in range(2):
                    relu_hidden((r * 2, k + 1), (1 + k) % 2)
                    copy_out((r * 2, k), k, r * 16)
            relu_hidden((0, NCH - 1), (NCH - 1) % 2)
            copy_out((0, NCH - 2), 0, (NCH - 2) * 8)
            copy_out((0, NCH - 1), 1, (NCH - 2) * 8)

            for i in range(GROUPS):
                for t in range(TG):
                    dve.wait_ge(gb_in[t], (i + 1) * (16 * TOPK))
                    if i or t >= 2:
                        dve.wait_ge(o_out[t % 2], i * (16 * TG // 2) + 16 * (t // 2))
                    for c in range(TOPK):
                        j = i * (TG * TOPK) + (t * TOPK + c)
                        if c:
                            dve.wait_ge(acc_done, j)
                        prev = ot[t % 2] if c else x1_sb[:, bass.ds(i * TG + t, 1), :].rearrange("p a d -> p (a d)")
                        v.scalar_tensor_tensor(out=ot[t % 2], in0=gb[:, t * TOPK + c, :], scalar=gates[:, bass.ds(j, 1)],
                                               in1=prev, op0=ALU.mult, op1=ALU.add).then_inc(acc_done, 1)

        @block.tensor
        def _(pe):
            t_ = nc.tensor

            pe.wait_ge(w_in, 16 * NSMALL)
            pe.wait_ge(ident_set, 1)
            for j in range(4):
                ins = t_.transpose(psB[0][:, j * D:(j + 1) * D], w_nat[:, j, :], ident[:])
            ins.then_inc(wT_ps, 1)
            for b in range(B):
                ins = t_.transpose(psM[:, b * S:(b + 1) * S], ctx_nat[:, b, :], ident[0:S, 0:S])
            ins.then_inc(ctxT_ps, 1)
            t_.transpose(psO[:, 0:NE], sel_nat, ident[0:NE, 0:NE]).then_inc(selT_ps, 1)
            pe.wait_ge(wkS_set, 1)
            pe.wait_ge(ctxT_sb, 1)
            for gi in range(NG):
                t_.matmul(psA[0:3 * HR, gi, 0:B * S].rearrange("p (b s) -> p b s", b=B),
                          wkS[:, gi].rearrange("p r c -> p (r c)"), ctxT[:, :, 0:S], start=True, stop=True
                          ).then_inc(kT_ps, 1)

            def project_v(b):
                for c in range(2):
                    t_.matmul(psB[b % 2][:, c * D:(c + 1) * D], ctxT[:, b, c * P:(c + 1) * P], wT[:, 2, :],
                              start=True, stop=True)
                for a in range(2):
                    ins = t_.matmul(psB[b % 2][64 * a:64 * a + 64, 2 * D:3 * D], ctxT[:, b, 2 * P:RP], wT[:, 2, :],
                                    start=True, stop=True)
                ins.then_inc(v_ps, 1)

            def transposes(src, dst, done):
                for t in range(T):
                    ins = t_.transpose(dst[:, t * P:(t + 1) * P], src[:, t, :], ident[:])
                ins.then_inc(done, 1)

            def turn_xn1(n):
                pe.wait_ge(xn1_ready, n + 1)
                if n:
                    pe.wait_ge(max_done, 2 * T * n)
                transposes(xn1, psA[:, NG - 1, :], xnT_ps)

            def project_q(n):
                pe.wait_ge(xnT_sb, n + 1)
                t_.matmul(psA[:, 2, :], wT[:, 0, :], xnT[:], start=True, stop=True).then_inc(q_ps, 1)

            def stack_q(n, k):
                pe.wait_ge(ql_sb, n + 1)
                for gi in range(NG):
                    t_.matmul(psA[:, gi, :], selq[:, gi, 0:4].rearrange("p r c -> p (r c)"), qh[:], start=True, stop=False)
                    t_.matmul(psA[:, gi, :], selq[:, gi, 2:6].rearrange("p r c -> p (r c)"), ql[:], start=False, stop=True
                              ).then_inc(stack_ps, 1)

            def scores_for_max(n, k, u):
                t, p = u // 2, u % 2
                if u == 0:
                    pe.wait_ge(kb_ready, n + 1)
                if u < 2:
                    pe.wait_ge(stack_sb, NG * n + 2 * p + 2)
                else:
                    pe.wait_ge(max_done, 2 * T * n + u - 1)
                for gi in range(2 * p, 2 * p + 2):
                    ins = t_.matmul(psA[:, gi, 0:R], qs[k][:, gi, t * P:(t + 1) * P], Ks[k][:, gi, 0:R],
                                    start=True, stop=True)
                ins.then_inc(a_ps, 1)

            def shift_rows(n):
                pe.wait_ge(split_lo, n + 1)
                for t in range(T):
                    ins = t_.transpose(mTp[:, t * P:(t + 1) * P],
                                       negm[:, t * NG:(t + 1) * NG, :].rearrange("p g j -> p (g j)"), identb[:])
                ins.then_inc(mT_ps, 1)

            def scores(n, k, v0, v1):
                for v in range(v0, v1):
                    p, j = v // 5, v % 5
                    g, c = 2 * p + j // 2, j % 2
                    if v == 0 or v == 2:
                        pe.wait_ge(mT_act, 2 * n + g + 1)
                    if v == 5 or v == 7:
                        pe.wait_ge(mT_dve, 2 * n + g - 1)
                    if n or v >= 2:
                        pe.wait_ge(exp_done, NU * n + v - 1)
                    if j < 4:
                        t_.matmul(psB[v % 2][:], Ks[k][:, g, c * P:(c + 1) * P], qs[k][:, g, :], start=True, stop=True
                                  ).then_inc(b_ps, 1)
                    else:
                        t_.matmul(psB[v % 2][:], KsT[k][:, 2 * p, :], qs[k][:, 2 * p, :], start=True, stop=False)
                        t_.matmul(psB[v % 2][:], KsT[k][:, 2 * p + 1, :], qs[k][:, 2 * p + 1, :],
                                  start=False, stop=True).then_inc(b_ps, 1)

            def attend(n, k, v):
                p, j = v // 5, v % 5
                if v == 0:
                    pe.wait_ge(exp_done, NU * (n + 1))
                    pe.wait_ge(vb_set, n + 1)
                if v == 5 and n:
                    pe.wait_ge(ex_done, n)
                ins = t_.matmul((psO, psM)[p][:], Vb[:, v].rearrange("p r c -> p (r c)"), PT[k][:, v, :],
                                start=(j == 0), stop=(j == 4))
                if j == 4:
                    ins.then_inc(o_ps, 1)

            def project_out(n):
                pe.wait_ge(att_done, 2 * n + 2)
                for t in range(T):
                    ins = t_.matmul(psM[:, t * D:(t + 1) * D], aT[:, t * P:(t + 1) * P], wT[:, 3, :], start=True, stop=True)
                ins.then_inc(y_ps, 1)

            def turn_xn2(n):
                pe.wait_ge(xn2_done, n + 1)
                pe.wait_ge(x1_done, n + 1)
                transposes(xn2_sb[:, n * T:(n + 1) * T], psM, xn2T_ps)

            def logits(n):
                pe.wait_ge(xn2T_sb, n + 1)
                for t in range(T):
                    ins = t_.matmul(psM[:, t * NE:(t + 1) * NE], xn2T[:, t * P:(t + 1) * P], selT[:], start=True, stop=True)
                ins.then_inc(lg_ps, 1)

            def count(i):
                pe.wait_ge(mask_done, BG * (i + 1))
                po = psA[:, 0, :].rearrange("p (t e) -> p t e", e=NE)
                t_.matmul(po, tri[:], mask[:], start=True, stop=False)
                for t in range(TG - 1):
                    t_.matmul(po[:, t + 1:TG, :], onesb[:], mask[:, t:t + 1, :].broadcast_to([P, TG - 1 - t, NE]),
                              start=False, stop=(t == TG - 2))
                for t in range(TG):
                    ins = t_.matmul(psA[:, 1, 0:NE], onesb[:], mask[:, t, :], start=(t == 0), stop=(t == TG - 1))
                ins.then_inc(route_ps, 1)

            def turn_table(i):
                pe.wait_ge(ej_done, i + 1)
                t_.matmul(psA[0:1, 2, 0:CAP], ej[0:CAP, 0:1], ident[0:CAP, 0:CAP], start=True, stop=True
                          ).then_inc(ejT_ps, 1)

            pe.wait_ge(kTf_set, NG)
            turn_xn1(0)
            pe.wait_ge(wT_sb, 1)
            project_q(0)
            pe.wait_ge(ctxT_zeroed, 1)
            for b in range(2):
                project_v(b)
            pe.wait_ge(selq_set, 2)
            stack_q(0, 0)
            for b in range(2, B):
                pe.wait_ge(vt_sb, b - 1)
                project_v(b)
            for u in range(2 * T):
                scores_for_max(0, 0, u)
            pe.wait_ge(identb_set, 1)
            pe.wait_ge(vt_sb, B)
            pe.wait_ge(kb_zeroed, BG)
            pe.wait_ge(selT_sb, 1)
            pe.wait_ge(tri_set, 1)
            pe.wait_ge(den_set, 2 * NG)
            for n in range(B + 2):
                k = n % 2
                more = n + 1 < B
                if more:
                    turn_xn1(n + 1)
                if n < B:
                    if n >= 2:
                        pe.wait_ge(att_done, 2 * (n - 1) - 1)
                    shift_rows(n)
                if n >= 2:
                    turn_xn2(n - 2)
                if more:
                    project_q(n + 1)
                if n >= 2:
                    logits(n - 2)
                if n >= BG + 1 and (n - 1) % BG == 0:
                    count((n - 1) // BG - 1)
                    turn_table((n - 1) // BG - 1)
                if n < B:
                    scores(n, k, 0, 2)
                    if n:
                        pe.wait_ge(mT_act, 2 * n + 2)
                        pe.wait_ge(mT_dve, 2 * n + 2)
                if n < B:
                    scores(n, k, 2, 3)
                if 1 <= n <= B:
                    attend(n - 1, 1 - k, 0)
                    attend(n - 1, 1 - k, 1)
                if more:
                    stack_q(n + 1, 1 - k)
                for u in range(2 * T):
                    if more:
                        scores_for_max(n + 1, 1 - k, u)
                    if 1 <= n <= B:
                        attend(n - 1, 1 - k, 2 + u)
                    if n < B and 3 + u < NU:
                        scores(n, k, 3 + u, 4 + u)
                if 1 <= n <= B:
                    project_out(n - 1)

            def numbers(m, chunks):
                _, vals = nc.values_load_multi_w_load_instructions(
                    etab[0:1, bass.ds(at(m) * CH, chunks * CH)], engines=(mybir.EngineType.PE,), min_val=0, max_val=NE - 1,
                    skip_runtime_bounds_check_because="the table's values are capped where it is written")
                return [vals[c * CH:(c + 1) * CH] for c in range(chunks)]

            def turn_rows(m, k, arrived):
                pe.wait_ge(xg_in[k], arrived)
                if not isinstance(m[0], int) or m[1] >= 2:
                    pe.wait_ge(g_xT_sb, at(m, -1))
                for j in range(CH):
                    ins = t_.transpose(psA[:, k % 2, j * P:(j + 1) * P], xg[k][:, j, :], ident[:])
                ins.then_inc(g_xT_ps, 1)

            def times_keys(m, k, es):
                pe.wait_ge(g_xT_sb, at(m, 1))
                if not isinstance(m[0], int) or m[1] >= 2:
                    pe.wait_ge(g_h_sb, at(m, -1))
                for j in range(CH):
                    ins = t_.matmul(psA[:, 2 + k, j * P:(j + 1) * P], xT[k][:, j * P:(j + 1) * P],
                                    keys_sb[:, bass.ds(es[j], 1), :].rearrange("p a d -> p (a d)"), start=True, stop=True)
                ins.then_inc(g_h_ps, 1)

            def turn_hidden(m, k):
                pe.wait_ge(g_h_sb, at(m, 1))
                if not isinstance(m[0], int) or m[1] >= 2:
                    pe.wait_ge(g_hT_sb, at(m, -1))
                for j in range(CH):
                    ins = t_.transpose(psB[k][:, j * P:(j + 1) * P], hr[k][:, j * P:(j + 1) * P], ident[:])
                ins.then_inc(g_hT_ps, 1)

            def times_values(m, k, es):
                pe.wait_ge(g_hT_sb, at(m, 1))
                if not isinstance(m[0], int) or m[1] >= 2:
                    pe.wait_ge(g_y_sb, at(m, -1))
                for j in range(CH):
                    ins = t_.matmul((psO, psM)[k][:, j * D:(j + 1) * D], hT[k][:, j * P:(j + 1) * P],
                                    vals_sb[:, bass.ds(es[j], 1), :].rearrange("p a d -> p (a d)"), start=True, stop=True)
                ins.then_inc(g_y_ps, 1)

            pe.wait_ge(etab_done, GROUPS)
            pe.wait_ge(k_in, 16)
            pe.wait_ge(v_in, 16)
            turn_rows((0, 0), 0, 16)
            turn_rows((0, 1), 1, 16)
            es = numbers((0, 0), UN)
            times_keys((0, 0), 0, es[0])
            turn_hidden((0, 0), 0)

            def step(m, arrived, es_before, es_now):
                base, off = m
                turn_rows((base, off + 1), (off + 1) % UN, arrived)
                times_keys(m, off % 2, es_now)
                times_values((base, off - 1), (off - 1) % 2, es_before)
                turn_hidden(m, off % 2)

            for m in range(1, UN):
                step((0, m), 16 * ((m + 1) // UN + 1), es[m - 1], es[m])
            with pe.Fori(1, NCH // UN - 1) as r:
                es = numbers((r * UN, -1), UN + 1)
                for u in range(UN):
                    step((r * UN, u), r * 16 + 16 * ((u + 1) // UN + 1), es[u], es[u + 1])
            es = numbers((0, NCH - UN - 1), UN + 1)
            for m in range(NCH - UN, NCH - 1):
                step((0, m), 16 * ((m + 1) // UN + 1), es[m % UN], es[m % UN + 1])
            m = (0, NCH - 1)
            times_keys(m, (NCH - 1) % 2, es[UN])
            times_values((0, NCH - 2), (NCH - 2) % 2, es[UN - 1])
            turn_hidden(m, (NCH - 1) % 2)
            times_values(m, (NCH - 1) % 2, es[UN])


_INS = ["x", "ctx_1024", "condB_tau", "fside_BxS2_0", "L0_xcond_Wq", "L0_xcond_bq", "L0_xcond_Wk", "L0_xcond_bk",
        "L0_xcond_Wv", "L0_xcond_bv", "L0_xcond_Wo", "L0_xcond_bo", "L0_ffn_expert_sel", "L0_ffn_keys", "L0_ffn_values"]


def kernel(**inputs):
    import numpy as _np
    import concourse.bacc as _bacc
    from concourse import mybir as _mybir
    from concourse.bass_utils import run_bass_kernel_spmd as _run

    nc = _bacc.Bacc("TRN2", target_bir_lowering=False, num_devices=1)
    arrays, args = {}, []
    for name in _INS:
        a = _np.ascontiguousarray(inputs[name])
        arrays[f"in_{name}_dram"] = a
        args.append(nc.dram_tensor(f"in_{name}_dram", a.shape, _mybir.dt.from_np(a.dtype), kind="ExternalInput").ap())
    args.append(nc.dram_tensor("out_0_dram", (B, L, D), F32, kind="ExternalOutput").ap())
    for name in ("sorted_rows", "result_rows"):
        args.append(nc.dram_tensor(name, (GROUPS * CAP * P, D), F32, kind="Internal").ap())
    block_kernel(nc, *args)
    r = _run(nc, [arrays], core_ids=[0])
    return r.results[0]["out_0_dram"]
```

```python
from contextlib import ExitStack

import concourse.bass as bass
from concourse import mybir

F32 = mybir.dt.float32
BF16 = mybir.dt.bfloat16
F32R = mybir.dt.float32r
I32 = mybir.dt.int32
U32 = mybir.dt.uint32
ALU = mybir.AluOpType
ACT = mybir.ActivationFunctionType
AX = mybir.AxisListType

P = 128
B, L, D = 4, 512, 128
S = 77
H, E = 16, 8
HG = 4
NG = H // HG
R = HG * S
TR = R - 2 * P
RP = 2 * P + P // 2
UP = 5
NU = NG // 2 * UP
HR = HG * E
T = L // P
NT = B * T
NE, TOPK = 64, 4
GROUP = (2, 2)
FIRST = [sum(GROUP[:i]) for i in range(len(GROUP) + 1)]
TG = [T * g for g in GROUP]
CAP = [t * TOPK + NE for t in TG]
TILE0 = [sum(CAP[:i]) for i in range(len(GROUP) + 1)]
CH = 4
NCH = TILE0[-1] // CH
UN = 4
EARLY = (4, 9)
SCALE = 1.0 / float(E) ** 0.5
EPS = 1e-5
ZW = 4


def block_kernel(nc, x, ctx_in, tau, fside, Wq, bq, Wk, bk, Wv, bv, Wo, bo, esel, keys, values, out, xs, ys):
    xf = x.rearrange("b l d -> (b l) d")
    of = out.rearrange("b l d -> (b l) d")

    with ExitStack() as stack:
        def sb(name, shape, dt=F32):
            return stack.enter_context(nc.sbuf_tensor(name, shape, dt))

        def sem(name):
            return stack.enter_context(nc.semaphore(name))

        x_sb = sb("x_sb", [P, NT, D])
        x1_sb = x_sb
        xn2_sb = sb("xn2_sb", [P, NT, D])
        keys_sb = sb("keys_sb", [P, NE, P])
        vals_sb = sb("vals_sb", [P, NE, D])
        wT = sb("wT", [P, 4, D])
        selT = sb("selT", [P, NE])
        bq_col = sb("bq_col", [P, 1])
        bkS = sb("bkS", [3 * HR, NG])
        bv_bc = sb("bv_bc", [P, D])
        bo_bc = sb("bo_bc", [P, D])
        tau_bc = sb("tau_bc", [P, B])
        K3 = sb("K3", [P, NG, B, S], F32R)
        vt = sb("vt", [P, B, 3, D])
        Vb = sb("Vb", [P, NU, 4, HR])

        ident = sb("ident", [P, P])
        identb = sb("identb", [P, P], BF16)
        onesf = sb("onesf", [P, P])
        onesb = sb("onesb", [P, P], BF16)
        tri = sb("tri", [P, P], BF16)
        onev = sb("onev", [P, 3, HG])
        vm0 = sb("vm0", [P, 3, HG])
        vm1 = sb("vm1", [P, HG])
        vm2 = sb("vm2", [P, HG])
        vmask = sb("vmask", [P, 4, HG])
        selq = sb("selq", [P, NG, 6, HR], F32R)
        pidx = sb("pidx", [P, 1], I32)
        pint = sb("pint", [P, 5], I32)
        pflt = sb("pflt", [P, 5])
        hrow = sb("hrow", [P, HG])
        hmask = sb("hmask", [P, HG])
        isd0 = sb("isd0", [P, 1])
        isd = sb("isd", [P, 1])
        rm = sb("rm", [P, 3])
        iota_e = sb("iota_e", [P, NE])
        jcol = sb("jcol", [P, 1])
        gbase = sb("gbase", [P, 1])
        zeros64 = sb("zeros64", [P, NE])
        mhalf = sb("mhalf", [P, T])
        zero = sb("zero", [P, ZW * D])

        st1 = sb("st1", [P, T, 6])
        mv1 = sb("mv1", [P, T, 2])
        ve1 = sb("ve1", [P, T])
        rs1 = sb("rs1", [P, T])
        xn1 = sb("xn1", [P, T, D])
        xnT = sb("xnT", [P, L])
        qf = xnT
        qh = sb("qh", [P, L], F32R)
        ql = sb("ql", [P, L], F32R)
        qs = [sb(f"qs{k}", [P, NG, L], F32R) for k in range(2)]
        Ks = [sb(f"Ks{k}", [P, NG, R], F32R) for k in range(2)]
        KsT = [sb(f"KsT{k}", [P, NG, P], F32R) for k in range(2)]
        mx = [sb(f"mx{k}", [P, T, H]) for k in range(2)]
        negm = sb("negm", [P, T * NG, HR], BF16)
        PT = [sb(f"PT{k}", [P, NU, L]) for k in range(2)]
        rden = sb("rden", [P, L])
        aT = sb("aT", [P, L])
        st2 = sb("st2", [P, T, 6])
        mv2 = sb("mv2", [P, T, 2])
        ve2 = sb("ve2", [P, T])
        rs2 = sb("rs2", [P, T])
        xn2T = sb("xn2T", [P, L])

        ex = sb("ex", [P, T, NE])
        wv = sb("wv", [P, T, NE])
        top = sb("top", [P, T, 8])
        tidx = sb("tidx", [P, T, 8], U32)
        tidf = sb("tidf", [P, T, 8])
        rgate = sb("rgate", [P, T, TOPK])
        gates = sb("gates", [P, NT * TOPK])
        OH = sb("OH", [P, max(TG), TOPK, NE], BF16)
        mask = sb("mask", [P, max(TG), NE], BF16)
        cnt_i = sb("cnt_i", [P, NE], I32)
        cnt_t = sb("cnt_t", [P, NE], I32)
        ntile = sb("ntile", [P, NE])
        incl = sb("incl", [P, NE])
        excl = sb("excl", [P, NE])
        sbase = sb("sbase", [P, NE])
        slotf = sb("slotf", [P, max(TG) * TOPK])
        slots = sb("slots", [P, NT * TOPK], I32)
        lecmp = sb("lecmp", [P, NE])
        ej = sb("ej", [P, len(GROUP)])
        etab = sb("etab", [1, TILE0[-1]], I32)

        pt0 = PT[0][:].rearrange("p v l -> p (v l)")
        pt1 = PT[1][:].rearrange("p v l -> p (v l)")
        o = 0
        w_nat = pt1[:, o:o + 4 * D].rearrange("p (j d) -> p j d", d=D)
        o += 4 * D
        ctx_nat = pt1[0:S, o:o + B * D].rearrange("p (b d) -> p b d", b=B)
        o += B * D
        sel_nat = pt1[0:NE, o:o + D]
        o += D
        KTf = pt1[:, o:o + NG * B * S].rearrange("p (g r) -> p g r", g=NG)
        o += NG * B * S
        tau_rep, delta_bc, dl, d3 = [pt1[:, o + j * B * S:o + (j + 1) * B * S] for j in range(4)]
        wkS = pt1[:, o + 5 * B * S:o + 5 * B * S + NG * 3 * HR].rearrange("p (g r c) -> p g r c", g=NG, r=3)
        dh = pt1[:, o + 4 * B * S:o + 5 * B * S].bitcast(F32R)
        ctxT = pt0[:, 0:B * RP].rearrange("p (b r) -> p b r", b=B)
        pos = pt0[:, 0:max(TG) * NE].rearrange("p (t e) -> p t e", e=NE)
        prod = pt0[:, 1024:2048].rearrange("p (t k e) -> p t k e", k=TOPK, e=NE)
        free = [pt0[:, t * TOPK * D:(t + 1) * TOPK * D] for t in range(8)]
        for used in (vt[:].rearrange("p b c d -> p (b c d)"), OH[:].rearrange("p t k e -> p (t k e)").bitcast(F32),
                     Vb[:].rearrange("p v r c -> p (v r c)"), rden[:]):
            free += [used[:, t * TOPK * D:(t + 1) * TOPK * D] for t in range(used.shape[1] // (TOPK * D))]
        gb = [place.rearrange("p (j d) -> p j d", d=D) for place in free[0:NT]]
        room = [pt1[:, j * CH * P:(j + 1) * CH * P] for j in range(NU)]
        room += [pt0[:, j * CH * P:(j + 1) * CH * P] for j in range(NU - 2, NU)]
        xg = [room[k].rearrange("p (a d) -> p a d", a=CH) for k in range(UN)]
        xT, ke, hT, yb = room[4:6], room[6:8], room[8:10], room[10:12]
        ot = [xn1[:, k, :] for k in range(2)]

        psA = stack.enter_context(nc.psum_tensor("psA", [P, NG, 512], F32))
        psB = [stack.enter_context(nc.psum_tensor(f"psB{k}", [P, 512], F32)) for k in range(2)]
        psO = stack.enter_context(nc.psum_tensor("psO", [P, 512], F32))
        psM = stack.enter_context(nc.psum_tensor("psM", [P, 512], F32))
        mTp = psO[:, 0:256].bitcast(BF16)

        x0_in, x_in, k_in, v_in = sem("x0_in"), sem("x_in"), sem("k_in"), sem("v_in")
        w_in = sem("w_in")
        b_in = sem("b_in")
        late_in = sem("late_in")
        zeroed = [sem(f"zeroed{g}") for g in range(len(GROUP))]
        scattered = [sem(f"scattered{g}") for g in range(len(GROUP))]
        ones_set = sem("ones_set")
        zero_set = sem("zero_set")
        ctxT_zeroed = sem("ctxT_zeroed")
        kb_zeroed = sem("kb_zeroed")
        negm_zeroed = sem("negm_zeroed")
        ident_set = sem("ident_set")
        identb_set = sem("identb_set")
        tri_set = sem("tri_set")
        small_set = sem("small_set")
        vm0_set = sem("vm0_set")
        vmask_set = sem("vmask_set")
        pint_set = sem("pint_set")
        pflt_set = sem("pflt_set")
        hmask_set = sem("hmask_set")
        rm_set = sem("rm_set")
        iota_set = sem("iota_set")
        wT_ps = sem("wT_ps")
        wT_sb = sem("wT_sb")
        ctxT_ps = sem("ctxT_ps")
        ctxT_sb = sem("ctxT_sb")
        selT_ps = sem("selT_ps")
        selT_sb = sem("selT_sb")
        wkT_ps = sem("wkT_ps")
        wkS_set = sem("wkS_set")
        isd_set = sem("isd_set")
        tau_set = sem("tau_set")
        dh_set = sem("dh_set")
        dl_set = sem("dl_set")
        d3_set = sem("d3_set")
        kT_ps = sem("kT_ps")
        kTf_set = sem("kTf_set")
        k3h_set = sem("k3h_set")
        k3_set = sem("k3_set")
        delta_set = sem("delta_set")
        v_ps = sem("v_ps")
        vt_sb = sem("vt_sb")
        vb_set = sem("vb_set")
        den_set = sem("den_set")
        xb_ready = sem("xb_ready")
        ln1_stats = sem("ln1_stats")
        ln1_aggr = sem("ln1_aggr")
        ln1_rstd = sem("ln1_rstd")
        xn1_ready = sem("xn1_ready")
        xnT_ps = sem("xnT_ps")
        xnT_sb = sem("xnT_sb")
        q_ps = sem("q_ps")
        qh_sb = sem("qh_sb")
        qf_sb = sem("qf_sb")
        stack_ps = sem("stack_ps")
        stack_sb = sem("stack_sb")
        rden_done = sem("rden_done")
        isd0_set = sem("isd0_set")
        selq_zeroed = sem("selq_zeroed")
        selq_set = sem("selq_set")
        vb_zeroed = sem("vb_zeroed")
        vm1_set = sem("vm1_set")
        vm2_set = sem("vm2_set")
        ql_sb = sem("ql_sb")
        kb_ready = sem("kb_ready")
        mT_sb = sem("mT_sb")
        ve_done = sem("ve_done")
        ve2_done = sem("ve2_done")
        a_ps = sem("a_ps")
        max_done = sem("max_done")
        split_hi = sem("split_hi")
        split_lo = sem("split_lo")
        mT_ps = sem("mT_ps")
        b_ps = sem("b_ps")
        exp_done = sem("exp_done")
        o_ps = sem("o_ps")
        att_done = sem("att_done")
        o_sb = sem("o_sb")
        y_ps = sem("y_ps")
        x1_done = sem("x1_done")
        ln2_stats = sem("ln2_stats")
        ln2_aggr = sem("ln2_aggr")
        ln2_rstd = sem("ln2_rstd")
        xn2_done = sem("xn2_done")
        xn2T_ps = sem("xn2T_ps")
        xn2T_sb = sem("xn2T_sb")
        lg_ps = sem("lg_ps")
        ex_done = sem("ex_done")
        w_done = sem("w_done")
        top_done = sem("top_done")
        idx_done = sem("idx_done")
        tidf_done = sem("tidf_done")
        rgate_done = sem("rgate_done")
        gates_done = sem("gates_done")
        oh_done = sem("oh_done")
        mask_done = sem("mask_done")
        route_ps = sem("route_ps")
        cnt_done = sem("cnt_done")
        shift_done = sem("shift_done")
        ntile_done = sem("ntile_done")
        incl_done = sem("incl_done")
        excl_done = sem("excl_done")
        base_done = sem("base_done")
        pos_done = sem("pos_done")
        prod_done = sem("prod_done")
        slotf_done = sem("slotf_done")
        slots_done = sem("slots_done")
        ej_done = sem("ej_done")
        ejT_ps = sem("ejT_ps")
        etab_done = sem("etab_done")
        step_done = sem("step_done")
        g_xT_ps = sem("g_xT_ps")
        g_xT_sb = sem("g_xT_sb")
        g_h_ps = sem("g_h_ps")
        g_h_sb = sem("g_h_sb")
        g_k_sb = sem("g_k_sb")
        g_y_ps = sem("g_y_ps")
        g_y_sb = sem("g_y_sb")
        acc_done = sem("acc_done")
        xg_in = [sem(f"xg_in{k}") for k in range(UN)]
        y_out = [sem(f"y_out{k}") for k in range(2)]
        gb_in = [sem(f"gb_in{k}") for k in range(NT)]
        o_out = [sem(f"o_out{k}") for k in range(2)]

        def at(m, d=0):
            return m[0] + (m[1] + d)

        def numbers(engine, m, chunks):
            _, vals = nc.values_load_multi_w_load_instructions(
                etab[0:1, bass.ds(at(m) * CH, chunks * CH)], engines=(engine,), min_val=0, max_val=NE - 1,
                skip_runtime_bounds_check_because="the table's values are capped where it is written")
            return [vals[c * CH:(c + 1) * CH] for c in range(chunks)]

        block = stack.enter_context(nc.Block())

        def load_rows(sp, m, k):
            sp.dma_start(xg[k], xs[bass.ds(at(m) * (CH * P), CH * P), :].rearrange("(a p) d -> p a d", p=P)
                         ).then_inc(xg_in[k], 16)

        def store_rows(sp, m, k):
            sp.wait_ge(g_y_sb, at(m, 1))
            sp.dma_start(ys[bass.ds(at(m) * (CH * P), CH * P), :].rearrange("(a p) d -> p a d", p=P),
                         yb[k].rearrange("p (a d) -> p a d", a=CH)).then_inc(y_out[k], 16)

        @block.sync
        def _(sp):
            xv = xf.rearrange("(t p) d -> p t d", p=P)
            sp.dma_start(x_sb[:, 0:T], xv[:, 0:T]).then_inc(x0_in, 16)
            sp.dma_start(w_nat[:, 1], Wk).then_inc(w_in, 16)
            sp.dma_start(ctx_nat, ctx_in.rearrange("b s d -> s b d")).then_inc(w_in, 16)
            for j, w in ((0, Wq), (2, Wv), (3, Wo)):
                sp.dma_start(w_nat[:, j], w).then_inc(w_in, 16)
            sp.dma_start(x_sb[:, T:NT], xv[:, T:NT]).then_inc(x_in, 16)
            sp.dma_start(sel_nat, esel).then_inc(late_in, 16)
            with nc.allow_non_contiguous_dma(reason="broadcast rows, small"):
                sp.dma_start(bv_bc[:], bv.rearrange("(a d) -> a d", a=1).broadcast_to([P, D])).then_inc(late_in, 16)
                sp.dma_start(bo_bc[:], bo.rearrange("(a d) -> a d", a=1).broadcast_to([P, D])).then_inc(late_in, 16)
            sp.wait_ge(zero_set, 1)
            zr = P * ZW
            half = CAP[0] * P // zr
            for j in range(half):
                sp.dma_start(xs[j * zr:(j + 1) * zr, :].rearrange("(p r) d -> p (r d)", p=P), zero[:]).then_inc(zeroed[0], 16)
            sp.dma_start(keys_sb[:], keys.rearrange("e d k -> d e k")).then_inc(k_in, 16)
            sp.dma_start(vals_sb[:], values.rearrange("e k v -> k e v")).then_inc(v_in, 16)
            for j in range(half, TILE0[-1] * P // zr):
                sp.dma_start(xs[j * zr:(j + 1) * zr, :].rearrange("(p r) d -> p (r d)", p=P), zero[:]).then_inc(zeroed[1], 16)
            sp.wait_ge(o_ps, 2 * B)
            for g in range(len(GROUP)):
                sp.wait_ge(scattered[g], 16 * TG[g] * TOPK)
                if g == 0:
                    for k in range(UN):
                        load_rows(sp, (0, k), k)
                    lo = 0
                else:
                    for k in range(UN):
                        m = TILE0[g] // CH - UN + k
                        sp.wait_ge(g_xT_ps, m + 1)
                        load_rows(sp, (0, m + UN), k)
                        store_rows(sp, (0, m), k % 2)
                    lo = TILE0[g] // CH
                hi = TILE0[g + 1] // CH - UN
                with sp.Fori(lo // UN, hi // UN) as r:
                    for k in range(UN):
                        sp.wait_ge(g_xT_ps, r * UN + (k + 1))
                        load_rows(sp, (r * UN, k + UN), k)
                        store_rows(sp, (r * UN, k), k % 2)
            for k in range(UN):
                store_rows(sp, (0, NCH - UN + k), k % 2)
            with sp.Fori(0, NT // 2) as r:
                t0 = r * 2
                for k in range(2):
                    sp.wait_ge(acc_done, t0 * TOPK + (k + 1) * TOPK)
                    sp.dma_start(of[bass.ds((t0 + k) * P, P), :], ot[k]).then_inc(o_out[k], 16)
            for k in range(2):
                sp.wait_ge(o_out[k], 16 * NT // 2)

        @block.gpsimd
        def _(pool):
            g = nc.gpsimd
            g.memset(onesf[:], 1.0).then_inc(ones_set, 1)
            g.memset(onev[:], 1.0).then_inc(ones_set, 1)
            g.memset(onesb[:], 1.0).then_inc(ones_set, 1)
            g.iota(pidx[:], pattern=[[0, 1]], base=0, channel_multiplier=1).then_inc(iota_set, 1)
            g.iota(iota_e[:], pattern=[[1, NE]], base=0, channel_multiplier=0,
                   allow_small_or_imprecise_dtypes=True).then_inc(iota_set, 1)
            g.iota(jcol[:], pattern=[[0, 1]], base=0, channel_multiplier=1,
                   allow_small_or_imprecise_dtypes=True).then_inc(iota_set, 1)
            g.iota(hrow[:], pattern=[[1, HG]], base=0, channel_multiplier=0,
                   allow_small_or_imprecise_dtypes=True).then_inc(iota_set, 1)
            g.memset(mhalf[:], -0.5).then_inc(small_set, 1)
            pool.wait_ge(ones_set, 3)
            g.affine_select(out=ident[:], in_=onesf[:], pattern=[[-1, P]], compare_op=ALU.is_equal, fill=0.0,
                            base=0, channel_multiplier=1).then_inc(ident_set, 1)
            g.memset(ctxT[:, :, R:RP], 0.0).then_inc(ctxT_zeroed, 1)
            g.affine_select(out=identb[:], in_=onesb[:], pattern=[[-1, P]], compare_op=ALU.is_equal, fill=0.0,
                            base=0, channel_multiplier=1).then_inc(identb_set, 1)
            g.memset(selq[:].bitcast(F32), 0.0).then_inc(selq_zeroed, 1)
            pool.wait_ge(ident_set, 1)
            pool.wait_ge(selq_zeroed, 1)
            eye = ident[:].rearrange("p (g c) -> p g () c", g=NG)
            g.tensor_copy(selq[:, :, 0:2, :], eye.broadcast_to([P, NG, 2, HR])).then_inc(selq_set, 1)
            g.tensor_copy(selq[:, :, 4:5, :], eye).then_inc(selq_set, 1)
            for k in range(2):
                g.memset(KsT[k][:].bitcast(F32), 0.0).then_inc(kb_zeroed, 1)
            g.memset(negm[:], 0.0).then_inc(negm_zeroed, 1)
            pool.wait_ge(negm_zeroed, 1)
            g.memset(negm[:, :, 2 * HG:2 * HG + 2], 1.0).then_inc(negm_zeroed, 1)
            g.affine_select(out=tri[:], in_=onesb[:], pattern=[[1, P]], compare_op=ALU.is_gt, fill=0.0,
                            base=0, channel_multiplier=-1).then_inc(tri_set, 1)
            g.memset(zeros64[:], 0.0).then_inc(small_set, 1)
            g.memset(gbase[:], 0.0).then_inc(small_set, 1)

            def spread_keys(n, k):
                pool.wait_ge(k3_set, 2 if n else 1)
                pool.wait_ge(delta_set, 1)
                pool.wait_ge(hmask_set, 2)
                if n >= 2:
                    pool.wait_ge(b_ps, NU * (n - 1))
                for gi in range(NG):
                    g.tensor_tensor(Ks[k][:, gi, 0:R].rearrange("p (h s) -> p h s", h=HG),
                                    K3[:, gi, n:n + 1, :].bitcast(F32).broadcast_to([P, HG, S]),
                                    hmask[:].rearrange("p h -> p h ()").broadcast_to([P, HG, S]), ALU.mult)
                for a in range(2):
                    ins = g.tensor_tensor(KsT[k][:].rearrange("p (b a) c -> p a b c", a=2)[:, a, :, 64 * a:64 * a + TR],
                                          K3[:].rearrange("p (b a) n s -> p a b n s", a=2)[:, a, :, n, S - TR:S].bitcast(F32),
                                          hmask[:, HG - 1:HG].rearrange("p h -> p h ()").broadcast_to([P, NG // 2, TR]),
                                          ALU.mult)
                ins.then_inc(kb_ready, 1)

            def rstd(n, ve, rs, eps, done):
                pool.wait_ge(eps, n + 1)
                g.tensor_tensor(rs[:], ve[:], mhalf[:], ALU.pow).then_inc(done, 1)

            def add_bo(n):
                pool.wait_ge(xn1_ready, n + 1)
                pool.wait_ge(late_in, 16 * 4)
                g.tensor_tensor(x_sb[:, n * T:(n + 1) * T, :], x_sb[:, n * T:(n + 1) * T, :],
                                bo_bc[:].rearrange("p d -> p () d").broadcast_to([P, T, D]), ALU.add
                                ).then_inc(xb_ready, 1)

            scatters = []

            def scatter(count):
                for _ in range(min(count, len(scatters))):
                    j = scatters.pop(0)
                    g.indirect_dma_start(out=xs[:, :], out_offset=bass.IndirectOffsetOnAxis(ap=slots[:, j:j + 1], axis=0),
                                         in_=xn2_sb[:, j // TOPK, :], in_offset=None).then_inc(scattered[j // (TG[0] * TOPK)], 16)

            def take_slots(i):
                pool.wait_ge(slots_done, i + 1)
                pool.wait_ge(xn2_done, FIRST[i + 1])
                pool.wait_ge(zeroed[i], 16 * CAP[i] // ZW)
                scatters.extend(FIRST[i] * T * TOPK + j for j in range(TG[i] * TOPK))

            def spread_values(b):
                pool.wait_ge(vt_sb, b + 1)
                if b:
                    pool.wait_ge(o_ps, 2 * b)
                for p in range(NG // 2):
                    for a in range(2):
                        cols = slice((2 * p + a) * HR, (2 * p + a + 1) * HR)
                        v0, tail = UP * p + 2 * a, UP * p + UP - 1
                        g.tensor_tensor(Vb[:, v0:v0 + 2, a, :].rearrange("p c (h e) -> p c h e", h=HG),
                                        vt[:, b, 0:2, cols].rearrange("p c (h e) -> p c h e", h=HG),
                                        vmask[:, 0:2, :].rearrange("p c h -> p c h ()").broadcast_to([P, 2, HG, E]),
                                        ALU.mult)
                        ins = g.tensor_tensor(Vb[:, tail:tail + 1, a, :].rearrange("p c (h e) -> p c h e", h=HG),
                                              vt[:, b, 2:3, cols].rearrange("p c (h e) -> p c h e", h=HG),
                                              vmask[:, 2 + a:3 + a, :].rearrange("p c h -> p c h ()"
                                                                                 ).broadcast_to([P, 1, HG, E]), ALU.mult)
                ins.then_inc(vb_set, 1)

            pool.wait_ge(small_set, 3)
            rstd(0, ve1, rs1, ve_done, ln1_rstd)
            g.affine_select(out=vm0[:], in_=onev[:], pattern=[[P, 3], [-S, HG]], compare_op=ALU.is_ge, fill=0.0,
                            base=0, channel_multiplier=1).then_inc(vm0_set, 1)
            g.affine_select(out=vm1[:], in_=onev[:, 0, :], pattern=[[-S, HG]], compare_op=ALU.is_ge, fill=0.0,
                            base=P + P // 2, channel_multiplier=1).then_inc(vm1_set, 1)
            pool.wait_ge(vm0_set, 1)
            g.affine_select(out=vmask[:, 0:3], in_=vm0[:], pattern=[[-P, 3], [S, HG]], compare_op=ALU.is_ge, fill=0.0,
                            base=S - 1, channel_multiplier=-1).then_inc(vmask_set, 1)
            pool.wait_ge(vm1_set, 1)
            g.affine_select(out=vm2[:], in_=vm1[:], pattern=[[S, HG]], compare_op=ALU.is_ge, fill=0.0,
                            base=S - 1 - P - P // 2, channel_multiplier=-1).then_inc(vm2_set, 1)
            pool.wait_ge(vm2_set, 1)
            g.affine_select(out=vmask[:, 3], in_=vm2[:], pattern=[[0, HG]], compare_op=ALU.is_ge, fill=0.0,
                            base=-(P // 2), channel_multiplier=1).then_inc(vmask_set, 1)
            g.memset(Vb[:], 0.0).then_inc(vb_zeroed, 1)
            pool.wait_ge(vmask_set, 2)
            pool.wait_ge(vb_zeroed, 1)
            for p in range(NG // 2):
                for a in range(2):
                    v0, tail = UP * p + 2 * a, UP * p + UP - 1
                    g.tensor_copy(Vb[:, v0:v0 + 2, 2 + a, :].rearrange("p c (h e) -> p c h e", h=HG),
                                  vmask[:, 0:2, :].rearrange("p c h -> p c h ()").broadcast_to([P, 2, HG, E])
                                  ).then_inc(den_set, 1)
                    g.tensor_copy(Vb[:, tail:tail + 1, 2 + a, :].rearrange("p c (h e) -> p c h e", h=HG),
                                  vmask[:, 2 + a:3 + a, :].rearrange("p c h -> p c h ()").broadcast_to([P, 1, HG, E])
                                  ).then_inc(den_set, 1)

            spread_keys(0, 0)
            add_bo(0)
            rstd(1, ve1, rs1, ve_done, ln1_rstd)
            spread_values(0)
            spread_keys(1, 1)
            add_bo(1)
            for n in range(B + 2):
                if 2 <= n + 1 < B:
                    spread_keys(n + 1, (n + 1) % 2)
                if 2 <= n <= B:
                    spread_values(n - 1)
                if n - 2 in FIRST[1:-1]:
                    take_slots(FIRST.index(n - 2) - 1)
                    scatter(EARLY[0])
                if n >= 2:
                    rstd(n - 2, ve2, rs2, ve2_done, ln2_rstd)
                scatter(EARLY[1] if n == B else len(scatters))
                if n + 2 < B:
                    rstd(n + 2, ve1, rs1, ve_done, ln1_rstd)
                    add_bo(n + 2)
            take_slots(len(GROUP) - 1)
            scatter(len(scatters))

            for j in range(NT * TOPK):
                grp = 0 if j < TG[0] * TOPK else 1
                if j in (0, TG[0] * TOPK):
                    for k in range(2):
                        pool.wait_ge(y_out[k], 16 * TILE0[grp + 1] // CH // 2)
                g.indirect_dma_start(out=gb[j // TOPK][:, j % TOPK, :], out_offset=None, in_=ys[0:TILE0[grp + 1] * P, :],
                                     in_offset=bass.IndirectOffsetOnAxis(ap=slots[:, j:j + 1], axis=0)
                                     ).then_inc(gb_in[j // TOPK], 16)

        @block.scalar
        def _(act):
            a = nc.scalar
            with nc.allow_non_contiguous_dma(reason="bias columns and broadcast rows, small"):
                for r in range(3):
                    act.dma_start(bkS[r * HR:(r + 1) * HR, :], bk.rearrange("(g p) -> p g", p=HR)).then_inc(b_in, 16)
                act.dma_start(tau_bc[:], tau.rearrange("(a d) -> a d", a=1).broadcast_to([P, B])).then_inc(b_in, 16)
                act.dma_start(delta_bc.rearrange("p (b s) -> p b s", b=B),
                              fside.rearrange("(a b) s -> a b s", a=1).broadcast_to([P, B, S])).then_inc(b_in, 16)
                act.dma_start(bq_col[:], bq.rearrange("(p a) -> p a", a=1)).then_inc(late_in, 16)
            act.wait_ge(wT_ps, 1)
            a.copy(wT[:, 0], psB[0][:, 0:D]).then_inc(wT_sb, 1)
            a.copy(wT[:, 2:4].rearrange("p j d -> p (j d)"), psB[0][:, 2 * D:4 * D]).then_inc(wT_sb, 1)
            act.wait_ge(late_in, 16 * 4)

            def copy_xnT(n):
                act.wait_ge(xnT_ps, n + 1)
                if n:
                    act.wait_ge(ql_sb, n)
                a.copy(xnT[:], psA[:, NG - 1, :]).then_inc(xnT_sb, 1)

            def copy_q(n):
                act.wait_ge(q_ps, n + 1)
                if n:
                    act.wait_ge(stack_ps, NG * n)
                a.activation(qh[:], psA[:, 2, :], ACT.Identity, bias=bq_col[:, 0:1]).then_inc(qh_sb, 1)
                a.activation(qf[:], psA[:, 2, :], ACT.Identity, bias=bq_col[:, 0:1]).then_inc(qf_sb, 1)

            def copy_stack(n, k):
                act.wait_ge(isd0_set, 2)
                for gi in range(NG):
                    act.wait_ge(stack_ps, NG * n + gi + 1)
                    a.activation(qs[k][:, gi, :], psA[:, gi, :], ACT.Identity, bias=isd0[:, 0:1]).then_inc(stack_sb, 1)

            def copy_shifts(n, k):
                act.wait_ge(mT_ps, n + 1)
                for gi in range(NG):
                    a.copy(qs[k][3 * HR:P, gi, :], mTp[gi * HR:(gi + 1) * HR, :]).then_inc(mT_sb, 1)

            def exps(n, k, v0, v1):
                for v in range(v0, v1):
                    act.wait_ge(b_ps, NU * n + v + 1)
                    a.activation(PT[k][:, v, :], psB[v % 2][:], ACT.Exp, scale=SCALE).then_inc(exp_done, 1)

            def copy_out_attention(n, p):
                act.wait_ge(o_ps, 2 * n + p + 1)
                if n and p == 0:
                    act.wait_ge(y_ps, n)
                rows = slice(2 * HR * p, 2 * HR * (p + 1))
                a.copy(rden[rows, :], psO[2 * HR:P, :]).then_inc(o_sb, 1)
                a.copy(aT[rows, :], psO[0:2 * HR, :]).then_inc(o_sb, 1)

            def copy_xn2T(n):
                act.wait_ge(xn2T_ps, n + 1)
                a.copy(xn2T[:], psM[:]).then_inc(xn2T_sb, 1)

            def exp_logits(n):
                act.wait_ge(lg_ps, n + 1)
                if n:
                    act.wait_ge(w_done, n)
                a.activation(ex[:].rearrange("p t e -> p (t e)"), psM[:, 0:T * NE], ACT.Exp,
                             scale=-1.0).then_inc(ex_done, 1)

            act.wait_ge(kTf_set, NG)
            for b0, b1 in ((0, 1), (1, B)):
                a.copy(K3[0:3 * HR, :, b0:b1].rearrange("p g b s -> p g (b s)"), KTf[0:3 * HR, :, b0 * S:b1 * S]
                       ).then_inc(k3h_set, 1)
            copy_xnT(0)
            copy_q(0)
            copy_stack(0, 0)
            for n in range(B + 2):
                k = n % 2
                more = n + 1 < B
                if more:
                    copy_xnT(n + 1)
                if n < B:
                    copy_shifts(n, k)
                if more:
                    copy_q(n + 1)
                if n < B:
                    exps(n, k, 0, 3)
                if more:
                    copy_stack(n + 1, 1 - k)
                if more:
                    exps(n, k, 3, 6)
                    if n:
                        copy_out_attention(n - 1, 0)
                    exps(n, k, 6, 8)
                    if n >= 2:
                        copy_xn2T(n - 2)
                    exps(n, k, 8, NU)
                    if n >= 2:
                        exp_logits(n - 2)
                    if n:
                        copy_out_attention(n - 1, 1)
                elif n < B:
                    exps(n, k, 3, 6)
                    copy_out_attention(n - 1, 0)
                    exps(n, k, 6, 7)
                    copy_xn2T(n - 2)
                    exps(n, k, 7, NU)
                    exp_logits(n - 2)
                    copy_out_attention(n - 1, 1)
                elif n == B:
                    copy_out_attention(n - 1, 0)
                    copy_out_attention(n - 1, 1)
                    copy_xn2T(n - 2)
                    exp_logits(n - 2)
                else:
                    copy_xn2T(n - 2)
                    exp_logits(n - 2)

            def copy_gxT(m, k):
                act.wait_ge(g_xT_ps, at(m, 1))
                a.copy(xT[k], psA[:, k, :]).then_inc(g_xT_sb, 1)

            def stage_keys(m, k, es):
                for j in range(CH):
                    ins = a.copy(ke[k][:, j * P:(j + 1) * P], keys_sb[:, bass.ds(es[j], 1), :].rearrange("p a d -> p (a d)"))
                ins.then_inc(g_k_sb, 1)

            act.wait_ge(etab_done, 1)
            act.wait_ge(k_in, 16)
            with act.Fori(0, NCH // UN) as r:
                es = numbers(mybir.EngineType.Activation, (r * UN, 0), UN)
                for u in range(UN):
                    copy_gxT((r * UN, u), u % 2)
                    stage_keys((r * UN, u), u % 2, es[u])

        @block.vector
        def _(dve):
            v = nc.vector
            v.memset(zero[:], 0.0).then_inc(zero_set, 1)
            dve.wait_ge(iota_set, 4)
            v.tensor_scalar(pint[:, 0:1], pidx[:], 3, 3, ALU.logical_shift_right, ALU.bitwise_and).then_inc(pint_set, 1)
            v.tensor_scalar(pint[:, 1:2], pidx[:], 31, None, ALU.bitwise_and).then_inc(pint_set, 1)
            v.tensor_scalar(pint[:, 2:3], pidx[:], 3, None, ALU.bitwise_and).then_inc(pint_set, 1)
            v.tensor_scalar(pint[:, 3:4], pidx[:], 1, 15, ALU.logical_shift_right, ALU.bitwise_and).then_inc(pint_set, 1)
            dve.wait_ge(pint_set, 4)
            v.tensor_copy(pflt[:, 0:4], pint[:, 0:4]).then_inc(pflt_set, 1)
            dve.wait_ge(pflt_set, 1)
            v.tensor_scalar(isd[:], pflt[:, 3:4], float(HG), None, ALU.is_equal).then_inc(isd_set, 1)
            v.memset(isd0[0:3 * HR], 0.0).then_inc(isd0_set, 1)
            v.tensor_scalar(isd0[3 * HR:P], pflt[3 * HR:P, 3:4], float(HG), None, ALU.is_equal).then_inc(isd0_set, 1)
            v.tensor_scalar(rm[:, 0:1], pflt[:, 1:2], float(2 * HG), None, ALU.is_equal).then_inc(rm_set, 1)
            v.tensor_scalar(rm[:, 1:2], pflt[:, 1:2], float(2 * HG + 1), None, ALU.is_equal).then_inc(rm_set, 1)
            v.tensor_scalar(rm[:, 2:3], pflt[:, 0:1], 0.0, None, ALU.is_equal).then_inc(rm_set, 1)
            v.tensor_scalar(hmask[0:3 * HR], hrow[0:3 * HR], pflt[0:3 * HR, 0:1], None, ALU.is_equal).then_inc(hmask_set, 1)
            dve.wait_ge(isd_set, 1)
            v.tensor_scalar(hmask[3 * HR:P], hrow[3 * HR:P], pflt[3 * HR:P, 2:3], isd[3 * HR:P, 0:1], ALU.is_equal,
                            ALU.max).then_inc(hmask_set, 1)

            def ln_stats(n, src, st, stats):
                for t in range(T):
                    ins = v.bn_stats(st[:, t, :], src(n, t))
                ins.then_inc(stats, 1)

            def ln_aggr(n, st, mv, ve, stats, aggr, eps):
                dve.wait_ge(stats, n + 1)
                for t in range(T):
                    ins = v.bn_aggr(mv[:, t, :], st[:, t, :])
                ins.then_inc(aggr, 1)
                dve.wait_ge(aggr, n + 1)
                v.tensor_scalar(ve[:], mv[:, :, 1:2].rearrange("p t a -> p (t a)"), EPS, None, ALU.add).then_inc(eps, 1)

            def ln_apply(n, src, dst, mv, rs, aggr, rstd_sem, done):
                dve.wait_ge(aggr, n + 1)
                dve.wait_ge(rstd_sem, n + 1)
                for t in range(T):
                    ins = v.tensor_scalar(dst[:, t, :], src(n, t), mv[:, t, 0:1], rs[:, t:t + 1], ALU.subtract, ALU.mult)
                ins.then_inc(done, 1)

            def x_tile(n, t):
                return x_sb[:, bass.ds(n * T + t, 1), :].rearrange("p a d -> p (a d)")

            def x1_tile(n, t):
                return x1_sb[:, bass.ds(n * T + t, 1), :].rearrange("p a d -> p (a d)")

            def norm1_stats(n):
                dve.wait_ge(x_in if n else x0_in, 16)
                ln_stats(n, x_tile, st1, ln1_stats)
                ln_aggr(n, st1, mv1, ve1, ln1_stats, ln1_aggr, ve_done)

            def norm1_apply(n):
                if n:
                    dve.wait_ge(xnT_ps, n)
                ln_apply(n, x_tile, xn1, mv1, rs1, ln1_aggr, ln1_rstd, xn1_ready)

            def low_q(n):
                dve.wait_ge(qh_sb, n + 1)
                dve.wait_ge(qf_sb, n + 1)
                if n:
                    dve.wait_ge(stack_ps, NG * n)
                v.tensor_tensor(ql[:], qf[:], qh[:].bitcast(F32), ALU.subtract).then_inc(ql_sb, 1)

            def maxima(n, k, u0, u1):
                for u in range(u0, u1):
                    t, p = u // 2, u % 2
                    dve.wait_ge(a_ps, 2 * T * n + u + 1)
                    v.tensor_reduce(mx[k][:, t, 8 * p:8 * p + 8].rearrange("p (a h) -> p a h", a=2),
                                    psA[:, 2 * p:2 * p + 2, 0:R].rearrange("p a (h s) -> p a h s", h=HG),
                                    AX.X, ALU.max).then_inc(max_done, 1)

            def split_max(n, k):
                dve.wait_ge(max_done, 2 * T * (n + 1))
                m = mx[k][:].rearrange("p t (g h) -> p (t g) h", g=NG)
                if n:
                    dve.wait_ge(mT_ps, n)
                v.tensor_scalar(negm[:, :, 0:HG], m, -1.0, None, ALU.mult).then_inc(split_hi, 1)
                dve.wait_ge(split_hi, n + 1)
                v.scalar_tensor_tensor(out=negm[:, :, HG:2 * HG], in0=m, scalar=-1.0, in1=negm[:, :, 0:HG],
                                       op0=ALU.mult, op1=ALU.subtract).then_inc(split_lo, 1)

            def normalise(n):
                dve.wait_ge(o_sb, 4 * n + 4)
                v.reciprocal(rden[:], rden[:]).then_inc(rden_done, 1)
                dve.wait_ge(rden_done, n + 1)
                v.tensor_tensor(aT[:], aT[:], rden[:], ALU.mult).then_inc(att_done, 1)

            def residual(n):
                dve.wait_ge(y_ps, n + 1)
                dve.wait_ge(xb_ready, n + 1)
                v.tensor_tensor(x1_sb[:, bass.ds(n * T, T), :], psM[:].rearrange("p (t d) -> p t d", t=T),
                                x_sb[:, bass.ds(n * T, T), :],
                                ALU.add).then_inc(x1_done, 1)

            def norm2_stats(n):
                dve.wait_ge(x1_done, n + 1)
                ln_stats(n, x1_tile, st2, ln2_stats)
                ln_aggr(n, st2, mv2, ve2, ln2_stats, ln2_aggr, ve2_done)

            def norm2_apply(n):
                ln_apply(n, x1_tile, xn2_sb[:, n * T:(n + 1) * T], mv2, rs2, ln2_aggr, ln2_rstd, xn2_done)

            def choose(n):
                dve.wait_ge(ex_done, n + 1)
                v.tensor_scalar(wv[:], ex[:], -1.0, -1.0, ALU.mult, ALU.add).then_inc(w_done, 1)
                dve.wait_ge(w_done, n + 1)
                for t in range(T):
                    ins = v.max(top[:, t, :], wv[:, t, :])
                ins.then_inc(top_done, 1)
                dve.wait_ge(top_done, n + 1)
                for t in range(T):
                    ins = v.max_index(tidx[:, t, :], top[:, t, :], wv[:, t, :])
                ins.then_inc(idx_done, 1)
                v.reciprocal(rgate[:], top[:, :, 0:TOPK]).then_inc(rgate_done, 1)
                dve.wait_ge(idx_done, n + 1)
                v.tensor_copy(tidf[:], tidx[:]).then_inc(tidf_done, 1)
                dve.wait_ge(tidf_done, n + 1)
                i = 0 if n < FIRST[1] else 1
                t0 = (n - FIRST[i]) * T
                if i:
                    dve.wait_ge(prod_done, FIRST[i])
                    dve.wait_ge(route_ps, i)
                v.tensor_tensor(OH[:, t0:t0 + T], iota_e[:].rearrange("p e -> p () () e").broadcast_to([P, T, TOPK, NE]),
                                tidf[:, :, 0:TOPK].rearrange("p t k -> p t k ()").broadcast_to([P, T, TOPK, NE]),
                                ALU.is_equal).then_inc(oh_done, 1)
                dve.wait_ge(oh_done, n + 1)
                with nc.allow_low_precision(reason="sums of 0 and 1, at most 1: exact"):
                    v.tensor_reduce(mask[:, t0:t0 + T, :], OH[:, t0:t0 + T].rearrange("p t k e -> p t e k"), AX.X,
                                    ALU.add).then_inc(mask_done, 1)
                dve.wait_ge(rgate_done, n + 1)
                v.tensor_scalar(gates[:, bass.ds(n * (T * TOPK), T * TOPK)], rgate[:].rearrange("p t k -> p (t k)"),
                                -1.0, None, ALU.mult).then_inc(gates_done, 1)

            def route(i):
                dve.wait_ge(route_ps, i + 1)
                v.tensor_scalar(cnt_i[:], psA[:, 3, 0:NE], float(P - 1), None, ALU.add).then_inc(cnt_done, 1)
                dve.wait_ge(cnt_done, i + 1)
                v.tensor_scalar(cnt_t[:], cnt_i[:], 7, None, ALU.logical_shift_right).then_inc(shift_done, 1)
                dve.wait_ge(shift_done, i + 1)
                v.tensor_copy(ntile[:], cnt_t[:]).then_inc(ntile_done, 1)
                dve.wait_ge(ntile_done, i + 1)
                if i:
                    dve.wait_ge(step_done, 2 * i)
                v.tensor_tensor_scan(incl[:], ntile[:], zeros64[:], gbase[:, 0:1], ALU.add, ALU.add).then_inc(incl_done, 1)
                dve.wait_ge(incl_done, i + 1)
                c = CAP[i]
                v.tensor_scalar(lecmp[0:c, :], incl[0:c, :], jcol[0:c, 0:1], 0.0, ALU.is_le, ALU.add,
                                accum_out=ej[0:c, i:i + 1]).then_inc(ej_done, 1)
                v.tensor_tensor(excl[:], incl[:], ntile[:], ALU.subtract).then_inc(excl_done, 1)
                dve.wait_ge(excl_done, i + 1)
                v.tensor_scalar(sbase[:], excl[:], float(P), None, ALU.mult).then_inc(base_done, 1)
                dve.wait_ge(base_done, i + 1)
                v.tensor_tensor(pos[:, 0:TG[i], :],
                                psA[:, 0:2, :].rearrange("p a c -> p (a c)")[:, 0:TG[i] * NE].rearrange("p (t e) -> p t e", e=NE),
                                sbase[:].rearrange("p e -> p () e").broadcast_to([P, TG[i], NE]), ALU.add
                                ).then_inc(pos_done, 1)
                dve.wait_ge(pos_done, i + 1)
                for b in range(GROUP[i]):
                    done = FIRST[i] + b
                    if done:
                        dve.wait_ge(slotf_done, done)
                    v.tensor_tensor(prod, OH[:, b * T:(b + 1) * T],
                                    pos[:, b * T:(b + 1) * T].rearrange("p t e -> p t () e").broadcast_to([P, T, TOPK, NE]),
                                    ALU.mult).then_inc(prod_done, 1)
                    if done == B - 1:
                        dve.wait_ge(ejT_ps, len(GROUP))
                        v.tensor_scalar(etab[:], psA[0:1, 2, 0:TILE0[-1]], float(NE - 1), None, ALU.min
                                        ).then_inc(etab_done, 1)
                    dve.wait_ge(prod_done, done + 1)
                    v.tensor_reduce(slotf[:, b * T * TOPK:(b + 1) * T * TOPK], prod.rearrange("p t k e -> p (t k) e"),
                                    AX.X, ALU.add).then_inc(slotf_done, 1)
                dve.wait_ge(slotf_done, FIRST[i + 1])
                j0, nj = FIRST[i] * T * TOPK, TG[i] * TOPK
                v.tensor_copy(slots[:, j0:j0 + nj], slotf[:, 0:nj]).then_inc(slots_done, 1)
                if i + 1 < len(GROUP):
                    v.tensor_scalar(jcol[:], jcol[:], float(CAP[i]), None, ALU.add).then_inc(step_done, 1)
                    v.tensor_scalar(gbase[:], gbase[:], float(CAP[i]), None, ALU.add).then_inc(step_done, 1)

            norm1_stats(0)
            norm1_apply(0)
            dve.wait_ge(wkT_ps, 1)
            v.tensor_copy(wkS, psB[1][:, 0:D].rearrange("p (g c) -> p g () c", g=NG).broadcast_to([P, NG, 3, HR])
                          ).then_inc(wkS_set, 1)
            dve.wait_ge(ctxT_ps, 1)
            v.tensor_copy(ctxT[:, :, 0:S], psM[:, 0:B * S].rearrange("p (b s) -> p b s", b=B)).then_inc(ctxT_sb, 1)
            v.tensor_copy(ctxT[:, :, S:R].rearrange("p b (h s) -> p b h s", h=HG - 1),
                          psM[:, 0:B * S].rearrange("p (b s) -> p b () s", b=B).broadcast_to([P, B, HG - 1, S])
                          ).then_inc(ctxT_sb, 1)
            dve.wait_ge(b_in, 16 * 5)
            v.tensor_copy(tau_rep.rearrange("p (b s) -> p b s", b=B),
                          tau_bc[:].rearrange("p b -> p b ()").broadcast_to([P, B, S])).then_inc(tau_set, 1)
            dve.wait_ge(tau_set, 1)
            for gi in range(NG):
                dve.wait_ge(kT_ps, gi + 1)
                v.scalar_tensor_tensor(out=KTf[0:3 * HR, gi, :], in0=psA[0:3 * HR, gi, 0:B * S], scalar=bkS[:, gi:gi + 1],
                                       in1=tau_rep[0:3 * HR], op0=ALU.add, op1=ALU.mult).then_inc(kTf_set, 1)
            lastb = slice(3 * HR, P)
            v.tensor_copy(dh[lastb], delta_bc[lastb]).then_inc(dh_set, 1)
            dve.wait_ge(dh_set, 1)
            v.tensor_tensor(dl[lastb], delta_bc[lastb], dh[lastb].bitcast(F32), ALU.subtract).then_inc(dl_set, 1)
            dve.wait_ge(dl_set, 1)
            dve.wait_ge(rm_set, 3)
            v.tensor_scalar(d3[lastb], dl[lastb], rm[lastb, 1:2], rm[lastb, 2:3], ALU.mult, ALU.add).then_inc(d3_set, 1)
            dve.wait_ge(d3_set, 1)
            for gi in range(NG):
                ins = v.scalar_tensor_tensor(out=K3[lastb, gi].rearrange("p b s -> p (b s)"), in0=dh[lastb].bitcast(F32),
                                             scalar=rm[lastb, 0:1], in1=d3[lastb], op0=ALU.mult, op1=ALU.add)
            ins.then_inc(delta_set, 1)
            lows = slice(HR, 2 * HR)
            dve.wait_ge(kTf_set, NG)
            for i, (b0, b1) in enumerate(((0, 1), (1, B))):
                dve.wait_ge(k3h_set, i + 1)
                k3 = K3[lows, :, b0:b1].rearrange("p g b s -> p g (b s)")
                v.tensor_tensor(k3, KTf[lows, :, b0 * S:b1 * S], k3.bitcast(F32), ALU.subtract).then_inc(k3_set, 1)
            dve.wait_ge(selT_ps, 1)
            v.tensor_copy(selT[:], psO[:, 0:NE]).then_inc(selT_sb, 1)
            low_q(0)

            def values(b):
                dve.wait_ge(v_ps, b + 1)
                v.tensor_tensor(vt[:, b], psB[b % 2][:, 0:3 * D].rearrange("p (c d) -> p c d", c=3),
                                bv_bc[:].rearrange("p d -> p () d").broadcast_to([P, 3, D]), ALU.add
                                ).then_inc(vt_sb, 1)

            dve.wait_ge(late_in, 16 * 4)
            norm1_stats(1)
            values(0)
            values(1)
            dve.wait_ge(negm_zeroed, 2)
            maxima(0, 0, 0, 4)
            norm1_apply(1)
            maxima(0, 0, 4, 2 * T)
            split_max(0, 0)
            values(2)
            values(3)
            for n in range(B + 2):
                k = n % 2
                more = n + 1 < B
                if more:
                    low_q(n + 1)
                if more:
                    maxima(n + 1, 1 - k, 0, 2)
                if n >= 2:
                    residual(n - 2)
                    norm2_stats(n - 2)
                if more:
                    maxima(n + 1, 1 - k, 2, 4)
                if n >= 2:
                    norm2_apply(n - 2)
                if n + 2 < B:
                    norm1_stats(n + 2)
                if more:
                    maxima(n + 1, 1 - k, 4, 6)
                if n + 2 < B:
                    norm1_apply(n + 2)
                if more:
                    maxima(n + 1, 1 - k, 6, 2 * T)
                    split_max(n + 1, 1 - k)
                if n in (B - 1, B + 1):
                    choose(n - 3)
                    choose(n - 2)
                if 1 <= n <= B:
                    normalise(n - 1)
                if n - 1 in FIRST[1:-1]:
                    route(FIRST.index(n - 1) - 1)
            route(len(GROUP) - 1)

            def relu_hidden(m, k):
                dve.wait_ge(g_h_ps, at(m, 1))
                v.tensor_scalar(hT[k], psA[:, 2 + k, :], 0.0, None, ALU.max).then_inc(g_h_sb, 1)

            def copy_out(m, k, stored):
                dve.wait_ge(g_y_ps, at(m, 1))
                if stored is not None:
                    dve.wait_ge(y_out[k], stored)
                v.tensor_copy(yb[k], (psO, psM)[k][:]).then_inc(g_y_sb, 1)

            relu_hidden((0, 0), 0)
            relu_hidden((0, 1), 1)
            copy_out((0, 0), 0, None)
            relu_hidden((0, 2), 0)
            copy_out((0, 1), 1, None)
            with dve.Fori(1, (NCH - 2) // 2) as r:
                for k in range(2):
                    relu_hidden((r * 2, k + 1), (1 + k) % 2)
                    copy_out((r * 2, k), k, r * 16)
            relu_hidden((0, NCH - 1), (NCH - 1) % 2)
            copy_out((0, NCH - 2), 0, (NCH - 2) * 8)
            copy_out((0, NCH - 1), 1, (NCH - 2) * 8)

            dve.wait_ge(gates_done, B)
            for t in range(NT):
                dve.wait_ge(gb_in[t], 16 * TOPK)
                if t >= 2:
                    dve.wait_ge(o_out[t % 2], 16 * (t // 2))
                for c in range(TOPK):
                    j = t * TOPK + c
                    if c:
                        dve.wait_ge(acc_done, j)
                    prev = ot[t % 2] if c else x1_sb[:, t, :]
                    v.scalar_tensor_tensor(out=ot[t % 2], in0=gb[t][:, c, :], scalar=gates[:, j:j + 1],
                                           in1=prev, op0=ALU.mult, op1=ALU.add).then_inc(acc_done, 1)

        @block.tensor
        def _(pe):
            t_ = nc.tensor

            pe.wait_ge(w_in, 16 * 5)
            pe.wait_ge(ident_set, 1)
            t_.transpose(psB[1][:, 0:D], w_nat[:, 1, :], ident[:]).then_inc(wkT_ps, 1)
            for b in range(B):
                ins = t_.transpose(psM[:, b * S:(b + 1) * S], ctx_nat[:, b, :], ident[0:S, 0:S])
            ins.then_inc(ctxT_ps, 1)
            for j in (0, 2, 3):
                ins = t_.transpose(psB[0][:, j * D:(j + 1) * D], w_nat[:, j, :], ident[:])
            ins.then_inc(wT_ps, 1)
            pe.wait_ge(wkS_set, 1)
            pe.wait_ge(ctxT_sb, 1)
            for gi in range(NG):
                t_.matmul(psA[0:3 * HR, gi, 0:B * S].rearrange("p (b s) -> p b s", b=B),
                          wkS[:, gi].rearrange("p r c -> p (r c)"), ctxT[:, :, 0:S], start=True, stop=True
                          ).then_inc(kT_ps, 1)

            def project_v(b):
                for c in range(2):
                    t_.matmul(psB[b % 2][:, c * D:(c + 1) * D], ctxT[:, b, c * P:(c + 1) * P], wT[:, 2, :],
                              start=True, stop=True)
                for a in range(2):
                    ins = t_.matmul(psB[b % 2][64 * a:64 * a + 64, 2 * D:3 * D], ctxT[:, b, 2 * P:RP], wT[:, 2, :],
                                    start=True, stop=True)
                ins.then_inc(v_ps, 1)

            def transposes(src, dst, done):
                for t in range(T):
                    ins = t_.transpose(dst[:, t * P:(t + 1) * P], src[:, t, :], ident[:])
                ins.then_inc(done, 1)

            def turn_xn1(n):
                pe.wait_ge(xn1_ready, n + 1)
                if n:
                    pe.wait_ge(max_done, 2 * T * n)
                transposes(xn1, psA[:, NG - 1, :], xnT_ps)

            def project_q(n):
                pe.wait_ge(xnT_sb, n + 1)
                t_.matmul(psA[:, 2, :], wT[:, 0, :], xnT[:], start=True, stop=True).then_inc(q_ps, 1)

            def stack_q(n, k):
                pe.wait_ge(ql_sb, n + 1)
                for gi in range(NG):
                    t_.matmul(psA[:, gi, :], selq[:, gi, 0:4].rearrange("p r c -> p (r c)"), qh[:], start=True, stop=False)
                    t_.matmul(psA[:, gi, :], selq[:, gi, 2:6].rearrange("p r c -> p (r c)"), ql[:], start=False, stop=True
                              ).then_inc(stack_ps, 1)

            def scores_for_max(n, k, u):
                t, p = u // 2, u % 2
                if u == 0:
                    pe.wait_ge(kb_ready, n + 1)
                if u < 2:
                    pe.wait_ge(stack_sb, NG * n + 2 * p + 2)
                else:
                    pe.wait_ge(max_done, 2 * T * n + u - 1)
                for gi in range(2 * p, 2 * p + 2):
                    ins = t_.matmul(psA[:, gi, 0:R], qs[k][:, gi, t * P:(t + 1) * P], Ks[k][:, gi, 0:R],
                                    start=True, stop=True)
                ins.then_inc(a_ps, 1)

            def shift_rows(n):
                pe.wait_ge(split_lo, n + 1)
                for t in range(T):
                    ins = t_.transpose(mTp[:, t * P:(t + 1) * P],
                                       negm[:, t * NG:(t + 1) * NG, :].rearrange("p g j -> p (g j)"), identb[:])
                ins.then_inc(mT_ps, 1)

            def scores(n, k, v0, v1):
                for v in range(v0, v1):
                    p, j = v // UP, v % UP
                    g, c = 2 * p + j // 2, j % 2
                    if j in (0, 2):
                        pe.wait_ge(mT_sb, NG * n + g + 1)
                    if n or v >= 2:
                        pe.wait_ge(exp_done, NU * n + v - 1)
                    if j < UP - 1:
                        t_.matmul(psB[v % 2][:], Ks[k][:, g, c * P:(c + 1) * P], qs[k][:, g, :], start=True, stop=True
                                  ).then_inc(b_ps, 1)
                    else:
                        t_.matmul(psB[v % 2][:], KsT[k][:, 2 * p, :], qs[k][:, 2 * p, :], start=True, stop=False)
                        t_.matmul(psB[v % 2][:], KsT[k][:, 2 * p + 1, :], qs[k][:, 2 * p + 1, :],
                                  start=False, stop=True).then_inc(b_ps, 1)

            def attend(n, k, v):
                p, j = v // UP, v % UP
                if v == 0:
                    pe.wait_ge(exp_done, NU * (n + 1))
                    pe.wait_ge(vb_set, n + 1)
                    if n:
                        pe.wait_ge(o_sb, 4 * n)
                if v == UP:
                    pe.wait_ge(o_sb, 4 * n + 2)
                ins = t_.matmul(psO[:], Vb[:, v].rearrange("p r c -> p (r c)"), PT[k][:, v, :],
                                start=(j == 0), stop=(j == UP - 1))
                if j == UP - 1:
                    ins.then_inc(o_ps, 1)

            def project_out(n):
                pe.wait_ge(att_done, n + 1)
                if n:
                    pe.wait_ge(ex_done, n)
                for t in range(T):
                    ins = t_.matmul(psM[:, t * D:(t + 1) * D], aT[:, t * P:(t + 1) * P], wT[:, 3, :], start=True, stop=True)
                ins.then_inc(y_ps, 1)

            def turn_xn2(n):
                pe.wait_ge(xn2_done, n + 1)
                pe.wait_ge(x1_done, n + 1)
                transposes(xn2_sb[:, n * T:(n + 1) * T], psM, xn2T_ps)

            def logits(n):
                pe.wait_ge(xn2T_sb, n + 1)
                for t in range(T):
                    ins = t_.matmul(psM[:, t * NE:(t + 1) * NE], xn2T[:, t * P:(t + 1) * P], selT[:], start=True, stop=True)
                ins.then_inc(lg_ps, 1)

            def count(i):
                pe.wait_ge(mask_done, FIRST[i + 1])
                for bank in range((TG[i] + 7) // 8):
                    t0, t1 = 8 * bank, min(8 * bank + 8, TG[i])
                    po = psA[:, bank, 0:(t1 - t0) * NE].rearrange("p (t e) -> p t e", e=NE)
                    t_.matmul(po, tri[:], mask[:, t0:t1], start=True, stop=False)
                    for t in range(t1 - 1):
                        t2 = max(t + 1, t0)
                        t_.matmul(po[:, t2 - t0:t1 - t0, :], onesb[:], mask[:, t:t + 1, :].broadcast_to([P, t1 - t2, NE]),
                                  start=False, stop=(t == t1 - 2))
                for t in range(TG[i]):
                    ins = t_.matmul(psA[:, 3, 0:NE], onesb[:], mask[:, t, :], start=(t == 0), stop=(t == TG[i] - 1))
                ins.then_inc(route_ps, 1)

            def turn_table(i):
                pe.wait_ge(ej_done, i + 1)
                t_.matmul(psA[0:1, 2, TILE0[i]:TILE0[i + 1]], ej[0:CAP[i], i:i + 1], ident[0:CAP[i], 0:CAP[i]],
                          start=True, stop=True).then_inc(ejT_ps, 1)

            pe.wait_ge(late_in, 16 * 4)
            t_.transpose(psO[:, 0:NE], sel_nat, ident[0:NE, 0:NE]).then_inc(selT_ps, 1)
            pe.wait_ge(kTf_set, NG)
            turn_xn1(0)
            pe.wait_ge(wT_sb, 2)
            project_q(0)
            pe.wait_ge(ctxT_zeroed, 1)
            pe.wait_ge(ctxT_sb, 2)
            for b in range(2):
                project_v(b)
            pe.wait_ge(selq_set, 2)
            stack_q(0, 0)
            for u in range(2 * T):
                scores_for_max(0, 0, u)
            for b in range(2, B):
                pe.wait_ge(vt_sb, b - 1)
                project_v(b)
            pe.wait_ge(identb_set, 1)
            pe.wait_ge(vt_sb, B)
            pe.wait_ge(kb_zeroed, 2)
            pe.wait_ge(selT_sb, 1)
            pe.wait_ge(tri_set, 1)
            pe.wait_ge(den_set, 2 * NG)
            for n in range(B + 2):
                k = n % 2
                more = n + 1 < B
                if more:
                    turn_xn1(n + 1)
                if n < B:
                    if n >= 2:
                        pe.wait_ge(o_sb, 4 * (n - 1))
                    shift_rows(n)
                if more:
                    project_q(n + 1)
                if n < B:
                    scores(n, k, 0, 2)
                    if n:
                        pe.wait_ge(mT_sb, NG * (n + 1))
                    scores(n, k, 2, 3)
                if 1 <= n <= B:
                    attend(n - 1, 1 - k, 0)
                    attend(n - 1, 1 - k, 1)
                if more:
                    stack_q(n + 1, 1 - k)
                if n >= 2:
                    project_out(n - 2)
                turn, lg = (4, 6) if n == B - 1 else (5, 7)
                for u in range(2 * T):
                    if more:
                        scores_for_max(n + 1, 1 - k, u)
                    if 2 <= n < B and u == turn:
                        turn_xn2(n - 2)
                    if n < B and 3 + u < NU:
                        scores(n, k, 3 + u, 4 + u)
                    if 2 <= n < B and u == lg:
                        logits(n - 2)
                    if 1 <= n <= B:
                        attend(n - 1, 1 - k, 2 + u)
                if n >= B:
                    turn_xn2(n - 2)
                    logits(n - 2)
                if n - 1 in FIRST[1:]:
                    i = FIRST.index(n - 1) - 1
                    if i:
                        pe.wait_ge(pos_done, i)
                    count(i)
            for i in range(len(GROUP)):
                turn_table(i)

            def turn_rows(m, k, arrived):
                pe.wait_ge(xg_in[k], arrived)
                if not isinstance(m[0], int) or m[1] >= 2:
                    pe.wait_ge(g_xT_sb, at(m, -1))
                for j in range(CH):
                    ins = t_.transpose(psA[:, k % 2, j * P:(j + 1) * P], xg[k][:, j, :], ident[:])
                ins.then_inc(g_xT_ps, 1)

            def times_keys(m, k):
                pe.wait_ge(g_xT_sb, at(m, 1))
                pe.wait_ge(g_k_sb, at(m, 1))
                if not isinstance(m[0], int) or m[1] >= 2:
                    pe.wait_ge(g_h_sb, at(m, -1))
                for j in range(CH):
                    ins = t_.matmul(psA[:, 2 + k, j * P:(j + 1) * P], ke[k][:, j * P:(j + 1) * P],
                                    xT[k][:, j * P:(j + 1) * P], start=True, stop=True)
                ins.then_inc(g_h_ps, 1)

            def times_values(m, k, es):
                pe.wait_ge(g_h_sb, at(m, 1))
                if not isinstance(m[0], int) or m[1] >= 2:
                    pe.wait_ge(g_y_sb, at(m, -1))
                for j in range(CH):
                    ins = t_.matmul((psO, psM)[k][:, j * D:(j + 1) * D], hT[k][:, j * P:(j + 1) * P],
                                    vals_sb[:, bass.ds(es[j], 1), :].rearrange("p a d -> p (a d)"), start=True, stop=True)
                ins.then_inc(g_y_ps, 1)

            pe.wait_ge(etab_done, 1)
            pe.wait_ge(k_in, 16)
            pe.wait_ge(v_in, 16)
            turn_rows((0, 0), 0, 16)
            turn_rows((0, 1), 1, 16)
            es = numbers(mybir.EngineType.PE, (0, 0), UN)
            times_keys((0, 0), 0)

            def step(m, arrived, es_before):
                base, off = m
                turn_rows((base, off + 1), (off + 1) % UN, arrived)
                times_keys(m, off % 2)
                times_values((base, off - 1), (off - 1) % 2, es_before)

            for m in range(1, UN):
                step((0, m), 16 * ((m + 1) // UN + 1), es[m - 1])
            with pe.Fori(1, NCH // UN - 1) as r:
                es = numbers(mybir.EngineType.PE, (r * UN, -1), UN + 1)
                for u in range(UN):
                    step((r * UN, u), r * 16 + 16 * ((u + 1) // UN + 1), es[u])
            es = numbers(mybir.EngineType.PE, (0, NCH - UN - 1), UN + 1)
            for m in range(NCH - UN, NCH - 1):
                step((0, m), 16 * ((m + 1) // UN + 1), es[m % UN])
            m = (0, NCH - 1)
            times_keys(m, (NCH - 1) % 2)
            times_values((0, NCH - 2), (NCH - 2) % 2, es[UN - 1])
            times_values(m, (NCH - 1) % 2, es[UN])


_INS = ["x", "ctx_1024", "condB_tau", "fside_BxS2_0", "L0_xcond_Wq", "L0_xcond_bq", "L0_xcond_Wk", "L0_xcond_bk",
        "L0_xcond_Wv", "L0_xcond_bv", "L0_xcond_Wo", "L0_xcond_bo", "L0_ffn_expert_sel", "L0_ffn_keys", "L0_ffn_values"]


def kernel(**inputs):
    import numpy as _np
    import concourse.bacc as _bacc
    from concourse import mybir as _mybir
    from concourse.bass_utils import run_bass_kernel_spmd as _run

    nc = _bacc.Bacc("TRN2", target_bir_lowering=False, num_devices=1)
    arrays, args = {}, []
    for name in _INS:
        a = _np.ascontiguousarray(inputs[name])
        arrays[f"in_{name}_dram"] = a
        args.append(nc.dram_tensor(f"in_{name}_dram", a.shape, _mybir.dt.from_np(a.dtype), kind="ExternalInput").ap())
    args.append(nc.dram_tensor("out_0_dram", (B, L, D), F32, kind="ExternalOutput").ap())
    for name in ("sorted_rows", "result_rows"):
        args.append(nc.dram_tensor(name, (TILE0[-1] * P, D), F32, kind="Internal").ap())
    block_kernel(nc, *args)
    r = _run(nc, [arrays], core_ids=[0])
    return r.results[0]["out_0_dram"]
```
